# Optimizing a Trainium2 kernel written in Bass

```python
import numpy as np
import jax
import jax.numpy as jnp

def _softmax(x, axis=-1):
    return jax.nn.softmax(x, axis=axis)

def _gelu(x):
    return jax.nn.gelu(x, approximate=True)

def _silu(x):
    return jax.nn.silu(x)

def _sigmoid(x):
    return jax.nn.sigmoid(x)

def _layernorm(x, axis=-1, eps=1e-05):
    m = jnp.mean(x, axis=axis, keepdims=True)
    v = jnp.var(x, axis=axis, keepdims=True)
    return (x - m) / jnp.sqrt(v + eps)

def _scatter_add(tgt, idx, src, axis=0):
    return tgt.at[idx].add(src)

def _segment_sum(src, seg, n):
    return jax.ops.segment_sum(src, seg, n)
kernel_name = 'mk_gnn_resnorm_d1_gnn_r8_334453'

def setup_inputs(seed: int=0):
    np.random.seed(seed)
    _w = jnp.asarray

    def _rec_inputs():
        import jax
        import jax.numpy as jnp
        _gk = jax.random.key(seed)
        x = -0.0002928 + 1 * jax.random.normal(jax.random.fold_in(_gk, 1), (6250, 256), jnp.float32)
        src = jax.random.randint(jax.random.fold_in(_gk, 2), (100000,), 0, 6250, jnp.int32)
        dst = jnp.minimum((6250 * jax.random.uniform(jax.random.fold_in(_gk, 3), (100000,)) ** 2.0).astype(jnp.int32), 49999)
        _o = jnp.argsort(dst, stable=True)
        src = src[_o]
        dst = dst[_o]
        edge_attr_256 = -5.72187e-05 + 0.999849 * jax.random.normal(jax.random.fold_in(_gk, 11), (100000, 256), jnp.float32)
        return (x, src, dst, edge_attr_256)
    x, src, dst, edge_attr_256 = _rec_inputs()

    def _L0_gnn_setup():
        import jax, jax.numpy as jnp
        import numpy as np
        HEADS = 8
        NEG_SLOPE = 0.2
        LN_EPS = 1e-05

        def _layernorm(x, g, b):
            m = jnp.mean(x, axis=-1, keepdims=True)
            v = jnp.var(x, axis=-1, keepdims=True)
            return (x - m) * jax.lax.rsqrt(v + LN_EPS) * g + b
        key = jax.random.key(seed)
        ks = jax.random.split(key, 12)
        N, E = (32768, 2048)
        D_NODE, D_EDGE_IN, D_EDGE = (256, 256, 256)
        H, C = (HEADS, D_EDGE // HEADS)
        s = lambda fan: 1.0 / np.sqrt(fan)
        return {'hyperedge': jax.random.normal(ks[0], (E, D_EDGE_IN), jnp.float32), 'hyper_node': jax.random.normal(ks[1], (N, D_NODE), jnp.float32), 've_affiliation': jax.random.randint(ks[2], (2, N), 0, E, dtype=jnp.int32), 'W_v2e': jax.random.normal(ks[3], (D_NODE, D_EDGE), jnp.float32) * s(D_NODE), 'b_v2e': jnp.zeros((D_EDGE,), jnp.float32), 'W_K': jax.random.normal(ks[4], (D_EDGE, D_EDGE), jnp.float32) * s(D_EDGE), 'b_K': jnp.zeros((D_EDGE,), jnp.float32), 'W_V': jax.random.normal(ks[5], (D_EDGE, D_EDGE), jnp.float32) * s(D_EDGE), 'b_V': jnp.zeros((D_EDGE,), jnp.float32), 'att_r': jax.random.normal(ks[6], (1, H, C), jnp.float32) * s(C), 'ln0_g': jnp.ones((D_EDGE,), jnp.float32), 'ln0_b': jnp.zeros((D_EDGE,), jnp.float32), 'ln1_g': jnp.ones((D_EDGE,), jnp.float32), 'ln1_b': jnp.zeros((D_EDGE,), jnp.float32), 'W_rff': jax.random.normal(ks[7], (D_EDGE, D_EDGE), jnp.float32) * s(D_EDGE), 'b_rff': jnp.zeros((D_EDGE,), jnp.float32), 'W_upd': jax.random.normal(ks[8], (D_EDGE + D_EDGE_IN, D_EDGE), jnp.float32) * s(D_EDGE + D_EDGE_IN), 'b_upd': jnp.zeros((D_EDGE,), jnp.float32)}
    _L0_gnn_all = _L0_gnn_setup()
    _L0_gnn_in = {k: v for k, v in _L0_gnn_all.items() if k in ('W_v2e', 'b_v2e', 'W_K', 'b_K', 'W_V', 'b_V', 'att_r', 'ln0_g', 'ln0_b', 'ln1_g', 'ln1_b', 'W_rff', 'b_rff', 'W_upd', 'b_upd')}
    del _L0_gnn_all
    return {'x': x, 'src': src, 'dst': dst, 'edge_attr_256': edge_attr_256, 'L0_gnn_W_v2e': _L0_gnn_in['W_v2e'], 'L0_gnn_b_v2e': _L0_gnn_in['b_v2e'], 'L0_gnn_W_K': _L0_gnn_in['W_K'], 'L0_gnn_b_K': _L0_gnn_in['b_K'], 'L0_gnn_W_V': _L0_gnn_in['W_V'], 'L0_gnn_b_V': _L0_gnn_in['b_V'], 'L0_gnn_att_r': _L0_gnn_in['att_r'], 'L0_gnn_ln0_g': _L0_gnn_in['ln0_g'], 'L0_gnn_ln0_b': _L0_gnn_in['ln0_b'], 'L0_gnn_ln1_g': _L0_gnn_in['ln1_g'], 'L0_gnn_ln1_b': _L0_gnn_in['ln1_b'], 'L0_gnn_W_rff': _L0_gnn_in['W_rff'], 'L0_gnn_b_rff': _L0_gnn_in['b_rff'], 'L0_gnn_W_upd': _L0_gnn_in['W_upd'], 'L0_gnn_b_upd': _L0_gnn_in['b_upd']}

def reference(x, src, dst, edge_attr_256, L0_gnn_W_v2e, L0_gnn_b_v2e, L0_gnn_W_K, L0_gnn_b_K, L0_gnn_W_V, L0_gnn_b_V, L0_gnn_att_r, L0_gnn_ln0_g, L0_gnn_ln0_b, L0_gnn_ln1_g, L0_gnn_ln1_b, L0_gnn_W_rff, L0_gnn_b_rff, L0_gnn_W_upd, L0_gnn_b_upd):
    import jax
    import jax.numpy as jnp

    def _L0_gnn_ref(hyperedge, hyper_node, ve_affiliation, W_v2e, b_v2e, W_K, b_K, W_V, b_V, att_r, ln0_g, ln0_b, ln1_g, ln1_b, W_rff, b_rff, W_upd, b_upd):
        import jax, jax.numpy as jnp
        import numpy as np
        HEADS = 8
        NEG_SLOPE = 0.2
        LN_EPS = 1e-05

        def _layernorm(x, g, b):
            m = jnp.mean(x, axis=-1, keepdims=True)
            v = jnp.var(x, axis=-1, keepdims=True)
            return (x - m) * jax.lax.rsqrt(v + LN_EPS) * g + b
        E = hyperedge.shape[0]
        seg = ve_affiliation[0]
        x = jax.nn.relu(hyper_node @ W_v2e + b_v2e)
        N, D = x.shape
        H, C = (HEADS, D // HEADS)
        xK = (x @ W_K + b_K).reshape(N, H, C)
        xV = (x @ W_V + b_V).reshape(N, H, C)
        alpha = jnp.sum(xK * att_r, axis=-1)
        alpha = jax.nn.leaky_relu(alpha, NEG_SLOPE)
        amax = jax.ops.segment_max(alpha, seg, num_segments=E)
        ex = jnp.exp(alpha - amax[seg])
        denom = jax.ops.segment_sum(ex, seg, num_segments=E)
        w = ex / jnp.maximum(denom[seg], 1e-16)
        out = jax.ops.segment_sum(xV * w[..., None], seg, num_segments=E)
        out = out + att_r
        out = out.reshape(E, D)
        out = _layernorm(out, ln0_g, ln0_b)
        out = _layernorm(out + jax.nn.relu(out @ W_rff + b_rff), ln1_g, ln1_b)
        hyperedge_tem = jax.nn.relu(out)
        cat = jnp.concatenate([hyperedge_tem, hyperedge], axis=-1)
        return jax.nn.relu(cat @ W_upd + b_upd)
    edge_index = jnp.stack([src, dst])
    x = _layernorm(x + _L0_gnn_ref(x, edge_attr_256, edge_index, L0_gnn_W_v2e, L0_gnn_b_v2e, L0_gnn_W_K, L0_gnn_b_K, L0_gnn_W_V, L0_gnn_b_V, L0_gnn_att_r, L0_gnn_ln0_g, L0_gnn_ln0_b, L0_gnn_ln1_g, L0_gnn_ln1_b, L0_gnn_W_rff, L0_gnn_b_rff, L0_gnn_W_upd, L0_gnn_b_upd), axis=-1)
    return x

_drawn_inputs = setup_inputs


def setup_inputs(seed=0):
    import zlib

    import numpy as np

    out = dict(_drawn_inputs(seed))
    spreads = {'L0_gnn_b_v2e': (0.0, 0.1),
     'L0_gnn_b_K': (0.0, 0.8),
     'L0_gnn_b_V': (0.0, 0.1),
     'L0_gnn_ln0_g': (1.0, 0.2),
     'L0_gnn_ln0_b': (0.0, 0.1),
     'L0_gnn_ln1_g': (1.0, 0.2),
     'L0_gnn_ln1_b': (0.0, 0.1),
     'L0_gnn_b_rff': (0.0, 0.408),
     'L0_gnn_b_upd': (0.0, 0.1)}
    factors = {}
    for name, (base, spread) in spreads.items():
        noise = np.random.default_rng([zlib.crc32(name.encode()), seed]).standard_normal(out[name].shape)
        drawn = base * np.exp(spread * noise) if base else spread * noise
        out[name] = jnp.asarray(drawn.astype(out[name].dtype))
    for name, factor in factors.items():
        out[name] = (out[name] * factor).astype(out[name].dtype)
    return out
```

```python
import concourse.bass as bass
from concourse import mybir
from concourse.bass import ds
from contextlib import ExitStack

FP32 = mybir.dt.float32
BF16 = mybir.dt.bfloat16
I16 = mybir.dt.int16
I32 = mybir.dt.int32
ALU = mybir.AluOpType
ACT = mybir.ActivationFunctionType
AX = mybir.AxisListType

P = 128
D = 256
KC = D // P
H = 8
C = D // H
EPS = 1e-5
SLOPE = 0.2
DENOM_MIN = 1e-16
SPAN = 30.0
FAR = -float(2 ** 100)

T = 4
BLOCK = T * P
VA = D + H
ROW = VA + 1
BANK = 512


def gnn_kernel(nc, x, src, edge, W_v2e, b_v2e, W_K, b_K, W_V, b_V, att_r, ln0_g, ln0_b, ln1_g,
               ln1_b, W_rff, b_rff, W_upd, b_upd, out):
    n_seg = x.shape[0]
    n_edge = edge.shape[0]
    n_block = -(-n_edge // BLOCK)
    last_start = n_edge - BLOCK
    repeated = (n_block - 1) * BLOCK - last_start
    n_tile = n_block * T
    n_bin = -(-n_seg // P)
    half = n_block // 2
    n_step = -(-(n_block + n_bin - 1) // 4) * 4
    n_row = n_block * BLOCK
    assert n_block % 2 == 0 and half <= P and repeated % T == 0
    batch = 7
    n_batch = n_bin // batch
    assert n_batch * batch == n_bin
    short = n_seg - (n_bin - 1) * P

    rows = nc.dram_tensor("binned_rows", (n_row, ROW), FP32).ap()
    rows_g = rows.rearrange("(g p t) d -> g p (t d)", p=P, t=T)
    rows_m = rows.rearrange("(g p t) d -> g p t d", p=P, t=T)
    edge_b = edge[0:(n_block - 1) * BLOCK, :].rearrange("(b p t) d -> b p (t d)", p=P, t=T)
    edge_last = edge[last_start:n_edge, :].rearrange("(p t) d -> p (t d)", t=T)

    ctx = ExitStack()
    with ctx:
        def sb(name, shape, dt=FP32):
            return ctx.enter_context(nc.sbuf_tensor(name, shape, dt))

        def sem(name):
            return ctx.enter_context(nc.semaphore(name))

        w_in = sb("w_in", [P, KC, D])
        w_k = sb("w_k", [P, KC, D])
        w_va = sb("w_va", [P, KC, VA])
        w_rff = sb("w_rff", [P, KC, D])
        w_upd = sb("w_upd", [P, 2 * KC, D])
        b_in = sb("b_in", [P, KC])
        b_in_rows = sb("b_in_rows", [KC, P])
        att = sb("att", [P, D])
        b_k = sb("b_k", [P, D])
        b_va = sb("b_va", [P, VA])
        g0, c0 = sb("g0", [P, D]), sb("c0", [P, D])
        g1, c1 = sb("g1", [P, D]), sb("c1", [P, D])
        brff, bupd = sb("brff", [P, D]), sb("bupd", [P, D])
        fold = sb("fold", [P, KC + 1, D])
        col = sb("col", [P, P])
        diff = sb("diff", [P, P])
        ident = sb("ident", [P, P])
        before = sb("before", [P, P])
        upto = sb("upto", [P, P])
        ones = sb("ones", [P, P])
        eps = sb("eps", [P, 1])
        step_no = sb("step_no", [P, n_step])
        far_ident = sb("far_ident", [P, P], BF16)
        hot = sb("hot", [P, 2, T, P])
        hot_t = sb("hot_t", [P, 2, T, P])
        src_i = hot[:, :, :, :].rearrange("p v t e -> p v (t e)").bitcast(I32)
        src_f = hot_t[:, :, :, :].rearrange("p v t e -> p v (t e)")
        seg_f = sb("seg_f", [P, n_block, T])
        seg_i = sb("seg_i", [P, n_tile], I32)
        bin_i = sb("bin_i", [P, n_tile], I32)
        bin_h = sb("bin_h", [P, n_tile], BF16)
        sums_w, load_w = (n_bin + 1) * VA, 4 * T * ROW
        early = sb("early", [P, max(n_bin * n_tile // 2, sums_w + load_w)])
        mask = early[:, 0:n_bin * n_tile // 2].bitcast(I16).rearrange("p (b t) -> p b t", b=n_bin)
        acc = early[:, 0:sums_w].rearrange("p (b v) -> p b v", v=VA)
        loaded = early[:, sums_w:sums_w + load_w].rearrange("p (u t d) -> p u t d", u=4, t=T)
        spare = sb("spare", [P, 2, n_tile], BF16)
        count = sb("count", [P, n_bin])
        total = sb("total", [P, n_bin])
        upto_bin = sb("upto_bin", [P, n_bin])
        start_at = sb("start_at", [P, n_bin])
        place = sb("place", [P, n_tile])
        place_i = sb("place_i", [P, n_tile], I32)
        tot_c = sb("tot_c", [P, 1])
        ends = sb("ends", [P, 4])
        ends_i = sb("ends_i", [P, 8], I32)
        mid = sb("mid", [P, 1])
        steps_c = sb("steps_c", [P, 1])
        steps_in = sb("steps_in", [P, 1])
        mid_w = sb("mid_w", [P, P])
        passed = sb("passed", [P, n_step])
        bin_of = sb("bin_of", [P, n_step])
        first_seg = sb("first_seg", [P, n_step])
        group_of = sb("group_of", [P, n_step])
        bin_of_i = sb("bin_of_i", [P, n_step], I32)
        group_of_i = sb("group_of_i", [P, n_step], I32)
        late = sb("late", [P, 12544])
        free = [0]

        def take(*shape):
            n = 1
            for k in shape:
                n *= k
            free[0] += n
            assert free[0] <= 12544
            v = late[:, free[0] - n:free[0]]
            names = "abc"[:len(shape)]
            if len(shape) == 1:
                return v
            return v.rearrange(f"p ({' '.join(names)}) -> p {' '.join(names)}",
                               **{m: k for m, k in zip(names, shape)})

        e_in = take(2, T * D)
        e_t = take(2, KC, BLOCK)
        x_t = take(2, KC, BLOCK)
        row = take(2, T, ROW)
        free[0] = 0
        y = take(batch, D)
        z = take(batch, D)
        xr_slot = take(batch, D)
        y_t = take(batch * KC, P)
        xr_t = take(batch * KC, P)
        res = take(batch, D)
        den = sb("den", [P, batch, H])
        rec = sb("rec", [P, batch, H])
        stats = sb("stats", [P, batch, 6])
        mv = sb("mv", [P, batch, 2])
        sd = sb("sd", [P, batch])
        rstd = sb("rstd", [P, batch])
        at = sb("at", [P, 2, T], I32)
        fill = row[:, 0, :, :].rearrange("p t d -> p (t d)")
        hi = sb("hi", [P, T, H])
        lo = sb("lo", [P, T, H])
        ext = sb("ext", [P, 2 * H])
        ext_all = sb("ext_all", [P, 2 * H])
        span = sb("span", [P, H])
        span1 = sb("span1", [P, 1])
        wide = sb("wide", [P, 1], I32)
        shift = sb("shift", [P, n_bin + 1, H])
        meta = sb("meta", [P, T, H + 1])
        seg_m = sb("seg_m", [P, T])
        outside = sb("outside", [P, T, P], BF16)
        spread = sb("spread", [P, H, P])
        seg_max = sb("seg_max", [P, H])
        pause = sb("pause", [P, 2])
        seg_r = sb("seg_r", [P, 2, T])
        off = sb("off", [P, 2, T, H])
        wv = sb("wv", [P, 2, T, VA])

        ps = ctx.enter_context(nc.psum_tensor("ps", [P, 8, BANK], FP32))

        params_in = sem("params_in")
        wk_in = sem("wk_in")
        src_in = sem("src_in")
        consts = sem("consts")
        folded = sem("folded")
        v_link = sem("v_link")
        src_cast = sem("src_cast")
        src_turned = sem("src_turned")
        masks_made = sem("masks_made")
        counted = sem("counted")
        totals_up = sem("totals_up")
        tot_c_up, tot_c_down = sem("tot_c_up"), sem("tot_c_down")
        ends_up = sem("ends_up")
        steps_down, steps_up = sem("steps_down"), sem("steps_up")
        passed_down, passed_up = sem("passed_down"), sem("passed_up")
        tables = sem("tables")
        filled, fill_set = sem("filled"), sem("fill_set")
        e_here = [sem("e_here0"), sem("e_here1")]
        e_turned, e_t_here = sem("e_turned"), sem("e_t_here")
        x_up, x_t_here = sem("x_up"), sem("x_t_here")
        va_up, va_taken = sem("va_up"), sem("va_taken")
        row_ready = sem("row_ready")
        v_score = sem("v_score")
        row_meta = sem("row_meta")
        sent = [sem("sent0"), sem("sent1")]
        ext_ready, ext_reduced, wide_known = sem("ext_ready"), sem("ext_reduced"), sem("wide_known")
        meta_in, meta_used = sem("meta_in"), sem("meta_used")
        v_max, outside_made, spread_made = sem("v_max"), sem("outside_made"), sem("spread_made")
        scores_up = sem("scores_up")
        shifts_known = sem("shifts_known")
        loaded_in = [sem(f"loaded_in{k}") for k in range(4)]
        seg_r_made, hot_made = sem("seg_r_made"), sem("hot_made")
        hot_turned, hot_t_here = sem("hot_turned"), sem("hot_t_here")
        shift_up = sem("shift_up")
        v_off, off_made, exp_made, wv_made = sem("v_off"), sem("off_made"), sem("exp_made"), sem("wv_made")
        sums_up, sums_added = sem("sums_up"), sem("sums_added")

        acc_clear = sem("acc_clear")
        b_in_turned, b_in_here = sem("b_in_turned"), sem("b_in_here")
        consts_made, runs_made, puts_made = sem("consts_made"), sem("runs_made"), sem("puts_made")
        normed = [sem(f"normed{n}") for n in range(3)]
        affine = [sem(f"affine{n}") for n in range(2)]
        p_link, v_link5 = sem("p_link"), sem("v_link5")
        var_ready, root_made = sem("var_ready"), sem("root_made")
        turned5, turned5_here = sem("turned5"), sem("turned5_here")
        z_ready, banks5_free, product_up = sem("z_ready"), sem("banks5_free"), sem("product_up")
        xr_here, xr_last, res_sent = sem("xr_here"), sem("xr_last"), sem("res_sent")

        params = [
            (w_in[:, :, :], W_v2e.rearrange("(k p) n -> p k n", p=P)),
            (w_va[:, :, 0:D], W_V.rearrange("(k p) n -> p k n", p=P)),
            (w_rff[:, :, :], W_rff.rearrange("(k p) n -> p k n", p=P)),
            (w_upd[:, :, :], W_upd.rearrange("(k p) n -> p k n", p=P)),
        ]
        rows_of = [(b_va[:, 0:D], b_V), (g0[:, :], ln0_g), (c0[:, :], ln0_b), (g1[:, :], ln1_g),
                   (c1[:, :], ln1_b), (brff[:, :], b_rff), (bupd[:, :], b_upd)]

        def every(v):
            return v.rearrange("(o n) -> o n", o=1).broadcast_to([P, v.shape[0]])

        with nc.Block() as block:

            @block.sync
            def _(sp):
                sp.dma_start(src_i[0:half, 0, :],
                             src[0:half * BLOCK].rearrange("(b n) -> b n", n=BLOCK)).then_inc(src_in, 16)
                sp.dma_start(src_i[0:half - 1, 1, :],
                             src[half * BLOCK:(n_block - 1) * BLOCK].rearrange("(b n) -> b n", n=BLOCK))\
                  .then_inc(src_in, 16)
                sp.dma_start(src_i[half - 1:half, 1, :],
                             src[last_start:n_edge].rearrange("(b n) -> b n", n=BLOCK)).then_inc(src_in, 16)
                for dst, of in params:
                    sp.dma_start(dst, of).then_inc(params_in, 16)
                for dst, of in rows_of:
                    sp.dma_start(dst, every(of)).then_inc(params_in, 16)
                def load_block(of, u):
                    sp.dma_start(e_in[:, u, :], of).then_inc(e_here[u], 16)
                load_block(edge_b[0], 0)
                load_block(edge_b[1], 1)
                with sp.Fori(1, n_block // 2 - 1) as t:
                    for u in range(2):
                        sp.wait_ge(e_turned, 2 * t + (u - 1))
                        load_block(edge_b[2 * t + u], u)
                sp.wait_ge(e_turned, n_block - 3)
                load_block(edge_b[n_block - 2], 0)
                sp.wait_ge(e_turned, n_block - 2)
                load_block(edge_last, 1)
                for u in range(2):
                    sp.wait_ge(sent[u], 16 * T * (n_block // 2))
                sp.wait_ge(filled, 16)
                sp.wait_ge(tables, 1)
                sp.wait_ge(wide_known, 1)
                far = sp.value_load(wide[0:1, 0:1], min_val=0, max_val=1)
                with sp.If(far > 0):
                    with sp.Fori(0, n_step) as i:
                        sp.wait_ge(meta_used, i + 1)
                        g = sp.value_load(group_of_i[0:1, ds(i, 1)], min_val=0, max_val=n_block - 1)
                        sp.dma_start(meta[:, :, :], rows_m[g][:, :, D:ROW]).then_inc(meta_in, 16)
                def load_step(i, u):
                    g = sp.value_load(group_of_i[0:1, ds(i, 1)], min_val=0, max_val=n_block - 1)
                    sp.dma_start(loaded[:, u, :, :].rearrange("p t d -> p (t d)"), rows_g[g])\
                      .then_inc(loaded_in[u], 16)
                for u in range(4):
                    load_step(u, u)
                with sp.Fori(1, n_step // 4) as q:
                    for u in range(4):
                        sp.wait_ge(wv_made, 4 * q + (u - 3))
                        load_step(4 * q + u, u)
                def batch_rows(t, k):
                    return t[0:(n_bin - 1) * P, :].rearrange("(b p) d -> p b d", p=P)[:, ds(k * batch, batch), :]
                sp.wait_ge(sums_added, n_step + 2)
                sp.nop().then_inc(res_sent, 16)
                with sp.Fori(0, n_batch - 1) as k:
                    sp.wait_ge(normed[2], k + 1)
                    sp.dma_start(xr_slot, batch_rows(x, k)).then_inc(xr_here, 16)
                    sp.wait_ge(normed[2], k + 2)
                    sp.dma_start(batch_rows(out, k), res).then_inc(res_sent, 16)
                full = (n_bin - 1) * P
                k = n_batch - 1
                sp.wait_ge(normed[2], n_batch)
                sp.dma_start(xr_slot[:, 0:batch - 1, :],
                             x[k * batch * P:full, :].rearrange("(b p) d -> p b d", p=P)).then_inc(xr_last, 16)
                sp.dma_start(xr_slot[0:short, batch - 1, :], x[full:n_seg, :]).then_inc(xr_last, 16)
                sp.wait_ge(xr_last, 32)
                sp.nop().then_inc(xr_here, 16)
                sp.wait_ge(normed[2], n_batch + 1)
                sp.dma_start(out[k * batch * P:full, :].rearrange("(b p) d -> p b d", p=P),
                             res[:, 0:batch - 1, :]).then_inc(res_sent, 16)
                sp.dma_start(out[full:n_seg, :], res[0:short, batch - 1, :]).then_inc(res_sent, 16)
                sp.wait_ge(res_sent, 16 * (n_batch + 2))

            @block.gpsimd
            def _(pool):
                pool.iota(col[:, :], [[1, P]], base=0, channel_multiplier=0,
                          allow_small_or_imprecise_dtypes=True).then_inc(consts, 1)
                pool.iota(diff[:, :], [[1, P]], base=0, channel_multiplier=-1,
                          allow_small_or_imprecise_dtypes=True).then_inc(consts, 1)
                pool.iota(step_no[:, :], [[1, n_step]], base=0, channel_multiplier=0,
                          allow_small_or_imprecise_dtypes=True).then_inc(consts, 1)
                pool.memset(ones[:, :], 1.0).then_inc(consts, 1)
                pool.memset(eps[:, :], EPS).then_inc(consts, 1)
                pool.memset(fill, float(P * (n_bin + 1))).then_inc(fill_set, 1)
                pool.wait_ge(fill_set, 1)
                pool.dma_start(rows[n_edge:n_row, :].rearrange("(p t) d -> p (t d)", t=T),
                               fill[0:(n_row - n_edge) // T, :]).then_inc(filled, 16)
                pool.wait_ge(filled, 16)
                pool.wait_ge(tables, 1)
                limit, bound = pool.alloc_register("limit"), pool.alloc_register("bound")
                pool.reg_mov(limit, n_row - 2)
                pool.reg_mov(bound, n_row - 1)

                def send(t, u):
                    if not isinstance(t, int):
                        pool.wait_ge(sent[u], 16 * T * t)
                    pool.tensor_copy(at[:, u, :], place_i[:, ds((2 * t + u) * T, T)]).then_inc(row_meta, 1)
                    pool.tensor_copy(row[:, u, :, VA:ROW],
                                     seg_f[:, ds(2 * t + u, 1), :].rearrange("p o t -> p t o"))\
                        .then_inc(row_meta, 1)
                    pool.wait_ge(row_ready, 2 * t + u + 1)
                    pool.wait_ge(row_meta, 4 * t + 2 * u + 2)
                    pool.reg_add(bound, limit, 1)
                    for j in range(T):
                        pool.indirect_dma_start(
                            rows, bass.IndirectOffsetOnAxis(ap=at[:, u, j:j + 1], axis=0),
                            row[:, u, j, :], None, bounds_check=bound, oob_is_err=False)\
                            .then_inc(sent[u], 16)

                for u in range(2):
                    send(0, u)
                with pool.Fori(1, n_block // 2) as t:
                    for u in range(2):
                        send(t, u)
                pool.wait_ge(ext_ready, 1)
                pool.partition_all_reduce(ext_all[:, :], ext[:, :], P, bass.bass_isa.ReduceOp.max)\
                    .then_inc(ext_reduced, 1)
                pool.memset(acc[:, :, :], 0.0).then_inc(acc_clear, 1)
                with pool.Fori(0, n_step // 4) as q:
                    for u in range(4):
                        i, v = 4 * q + u, u % 2
                        pool.wait_ge(sums_up, 4 * q + (u + 1))
                        pool.wait_ge(loaded_in[u], 16 * q + 16)
                        pool.tensor_tensor(seg_r[:, v, :], loaded[:, u, :, VA],
                                           first_seg[:, ds(i, 1)].to_broadcast([P, T]), ALU.subtract)\
                            .then_inc(seg_r_made, 1)
                        pool.wait_ge(seg_r_made, 4 * q + (u + 1))
                        pool.tensor_tensor(pause[:, 0:1], seg_r[:, v, 0:1], seg_r[:, v, 0:1], ALU.add)
                        for j in range(T):
                            last = pool.tensor_scalar(hot[:, v, j, :], col[:, :], seg_r[:, v, j:j + 1], None,
                                                      ALU.is_equal)
                        last.then_inc(hot_made, 1)
                with pool.Fori(0, n_batch) as k:
                    for n, (to, gain, bias) in enumerate(((y, g0, c0), (z, g1, c1))):
                        pool.wait_ge(normed[n], k + 1)
                        pool.tensor_tensor(to, to, gain[:, :].unsqueeze(1).to_broadcast([P, batch, D]),
                                           ALU.mult).then_inc(p_link, 1)
                        pool.wait_ge(p_link, 2 * k + (n + 1))
                        pool.tensor_tensor(to, to, bias[:, :].unsqueeze(1).to_broadcast([P, batch, D]),
                                           ALU.add).then_inc(affine[n], 1)

            @block.scalar
            def _(act):
                act.nop().then_inc(hot_t_here, 1)
                act.nop().then_inc(turned5_here, 1)
                act.dma_start(w_k[:, :, :], W_K.rearrange("(k p) n -> p k n", p=P)).then_inc(wk_in, 16)
                act.dma_start(att[:, :], every(att_r.rearrange("a h c -> (a h c)"))).then_inc(wk_in, 16)
                act.dma_start(b_k[:, :], every(b_K)).then_inc(wk_in, 16)
                act.dma_start(b_in_rows[:, :], b_v2e.rearrange("(k p) -> k p", p=P)).then_inc(wk_in, 16)
                act.wait_ge(b_in_turned, 1)
                act.activation(b_in[:, :], ps[:, 3, 0:KC], ACT.Copy).then_inc(b_in_here, 1)
                for b in range(n_bin):
                    act.wait_ge(masks_made, b + 1)
                    if b >= 2:
                        act.wait_ge(counted, b - 1)
                    act.activation(spare[:, b % 2, :], mask[:, b, :], ACT.Copy, accum_out=count[:, b:b + 1])\
                       .then_inc(counted, 1)

                def take_edges(i, v, n):
                    act.wait_ge(e_turned, n + 1)
                    act.wait_ge(x_up, n + 1)
                    for k in range(KC):
                        last = act.activation(e_t[:, v, k, :], ps[:, k, :], ACT.Copy)
                    last.then_inc(e_t_here, 1)

                def take_hidden(i, v, n):
                    act.wait_ge(x_up, n + 3)
                    act.wait_ge(va_up, n + 1)
                    for k in range(KC):
                        last = act.activation(x_t[:, v, k, :], ps[:, 2 + k, :], ACT.Relu,
                                              bias=b_in[:, k:k + 1])
                    last.then_inc(x_t_here, 1)

                act.wait_ge(b_in_here, 1)
                take_edges(0, 0, 0)
                with act.Fori(0, n_block // 2 - 1) as t:
                    for u in range(2):
                        take_edges(None, 1 - u, 2 * t + (u + 1))
                        take_hidden(None, u, 2 * t + u)
                take_edges(n_block - 1, 1, n_block - 1)
                take_hidden(n_block - 2, 0, n_block - 2)
                take_hidden(n_block - 1, 1, n_block - 1)

                def turned_hot(n, v):
                    act.wait_ge(hot_turned, n + 1)
                    act.wait_ge(shift_up, n + 1)
                    act.activation(hot_t[:, v, :, :], ps[:, v, :].rearrange("p (t e) -> p t e", t=T),
                                   ACT.Copy).then_inc(hot_t_here, 1)

                def exps(n, v):
                    act.wait_ge(off_made, n + 1)
                    act.wait_ge(sums_up, n + 1)
                    act.activation(wv[:, v, :, D:VA], off[:, v, :, :], ACT.Exp).then_inc(exp_made, 1)

                with act.Fori(0, n_step // 4) as q:
                    for u in range(4):
                        turned_hot(4 * q + u, u % 2)
                        if u:
                            exps(4 * q + (u - 1), (u - 1) % 2)
                    exps(4 * q + 3, 1)

                def root(n):
                    act.wait_ge(var_ready, n + 1)
                    act.activation(sd[:, :], mv[:, :, 1], ACT.Sqrt, bias=eps[:, 0:1]).then_inc(root_made, 1)

                def take_turned(to, n):
                    act.wait_ge(turned5, n + 1)
                    act.activation(to, ps[:, 0:4, :].rearrange("p a n -> p (a n)")[:, 0:batch * KC * P]
                                   .rearrange("p (a n) -> p a n", n=P), ACT.Copy).then_inc(turned5_here, 1)

                with act.Fori(0, n_batch) as k:
                    root(3 * k)
                    take_turned(xr_t, 3 * k)
                    take_turned(y_t, 3 * k + 1)
                    root(3 * k + 1)
                    act.wait_ge(affine[1], k + 1)
                    act.activation(z, z, ACT.Relu).then_inc(z_ready, 1)
                    take_turned(y_t, 3 * k + 2)
                    root(3 * k + 2)

            @block.tensor
            def _(pe):
                pe.nop().then_inc(x_up, 2)
                pe.nop().then_inc(va_up, 2)
                pe.nop().then_inc(sums_up, 2)
                pe.nop().then_inc(shift_up, 2)
                pe.wait_ge(consts_made, 1)
                pe.wait_ge(src_cast, 1)
                for s in range(2):
                    for j in range(T):
                        last = pe.transpose(
                            ps[:, s, j * half:(j + 1) * half],
                            src_f[0:half, s, :].rearrange("b (p t) -> b t p", t=T)[:, j, :],
                            ident[0:half, 0:half])
                last.then_inc(src_turned, 1)
                pe.wait_ge(wk_in, 64)
                pe.transpose(ps[:, 3, 0:KC], b_in_rows[:, :], ident[0:KC, 0:KC]).then_inc(b_in_turned, 1)
                pe.wait_ge(counted, n_bin)
                pe.wait_ge(b_in_here, 1)
                pe.matmul(ps[:, 2, 0:n_bin], before[:, :], count[:, :], start=True, stop=True)
                pe.matmul(ps[:, 2, 64:64 + n_bin], ones[:, :], count[:, :], start=True, stop=True)
                pe.matmul(ps[0:n_bin, 2, 128:129], count[:, :], ones[:, 0:1], start=True, stop=True)\
                  .then_inc(totals_up, 1)
                nb = n_bin
                pe.wait_ge(tot_c_down, 1)
                pe.matmul(ps[0:nb, 3, 16:17], upto[0:nb, 0:nb], tot_c[0:nb, :], start=True, stop=True)
                pe.matmul(ps[0:nb, 3, 17:18], before[0:nb, 0:nb], tot_c[0:nb, :], start=True, stop=True)\
                  .then_inc(ends_up, 1)
                pe.wait_ge(steps_down, 1)
                pe.matmul(ps[0:nb, 3, 32:33], upto[0:nb, 0:nb], steps_c[0:nb, :], start=True, stop=True)\
                  .then_inc(steps_up, 1)
                pe.wait_ge(passed_down, 1)
                pe.matmul(ps[:, 0, 0:n_step], ones[0:nb, :], passed[0:nb, :], start=True, stop=True)
                pe.matmul(ps[:, 1, 0:n_step], mid_w[0:nb, :], passed[0:nb, :], start=True, stop=True)\
                  .then_inc(passed_up, 1)
                pe.wait_ge(tables, 1)
                pe.wait_ge(params_in, 16 * (len(params) + len(rows_of)))

                def turn(u, here, n):
                    pe.wait_ge(e_here[u], here)
                    pe.wait_ge(e_t_here, n)
                    for k in range(KC):
                        for j in range(T):
                            at_ = j * D + k * P
                            last = pe.transpose(ps[:, k, j * P:(j + 1) * P], e_in[:, u, at_:at_ + P],
                                                ident[:, :])
                    last.then_inc(e_turned, 1)

                def hidden(u, n):
                    pe.wait_ge(e_t_here, n + 1)
                    pe.wait_ge(x_t_here, n)
                    for m in range(KC):
                        for k in range(KC):
                            last = pe.matmul(ps[:, 2 + m, :], w_in[:, k, m * P:(m + 1) * P], e_t[:, u, k, :],
                                             start=(k == 0), stop=(k == KC - 1))
                    last.then_inc(x_up, 1)

                def values(u, n):
                    pe.wait_ge(x_t_here, n + 1)
                    pe.wait_ge(va_taken, n + 1)
                    for j in range(T):
                        for k in range(KC):
                            last = pe.matmul(ps[:, 4 + j, 0:VA], x_t[:, u, k, j * P:(j + 1) * P], w_va[:, k, :],
                                             start=(k == 0), stop=(k == KC - 1))
                    last.then_inc(va_up, 1)

                turn(0, 16, 0)
                turn(1, 16, 1)
                hidden(0, 0)
                with pe.Fori(0, n_block // 2 - 1) as t:
                    for u in range(2):
                        turn(u, 16 * t + 32, 2 * t + (u + 2))
                        hidden(1 - u, 2 * t + (u + 1))
                        values(u, 2 * t + u)
                hidden(1, n_block - 1)
                values(0, n_block - 2)
                values(1, n_block - 1)

                pe.wait_ge(wide_known, 1)
                far = pe.value_load(wide[0:1, 0:1], min_val=0, max_val=1)
                with pe.If(far > 0):
                    with pe.Fori(0, n_step) as i:
                        for j in range(T):
                            pe.wait_ge(outside_made, i + 1)
                            pe.wait_ge(spread_made, T * i + (j + 1))
                            for g in range(2):
                                pe.matmul(ps[:, g, :], outside[:, j, :],
                                          far_ident[:, :].unsqueeze(1).to_broadcast([P, H // 2, P]),
                                          start=True, stop=False)
                                last = pe.matmul(ps[:, g, :], ones[:, :],
                                                 spread[:, g * H // 2:(g + 1) * H // 2, :],
                                                 start=False, stop=True)
                            last.then_inc(scores_up, 1)
                pe.wait_ge(shifts_known, 1)

                def turn_hot(n, v):
                    pe.wait_ge(hot_made, n + 1)
                    pe.wait_ge(hot_t_here, n + 1)
                    for j in range(T):
                        last = pe.transpose(ps[:, v, j * P:(j + 1) * P], hot[:, v, j, :], ident[:, :])
                    last.then_inc(hot_turned, 1)

                def edge_shifts(n, v, i):
                    b = pe.value_load(bin_of_i[0:1, ds(i, 1)], min_val=0, max_val=n_bin)
                    pe.wait_ge(hot_t_here, n + 2)
                    pe.wait_ge(v_off, n + 1)
                    for j in range(T):
                        last = pe.matmul(ps[:, 2 + v, j * H:(j + 1) * H], hot_t[:, v, j, :], shift[:, b, :],
                                         start=True, stop=True)
                    last.then_inc(shift_up, 1)

                def sums(n, v):
                    pe.wait_ge(wv_made, n + 1)
                    pe.wait_ge(sums_added, n + 1)
                    for j in range(T):
                        last = pe.matmul(ps[:, 4 + v, 0:VA], hot[:, v, j, :], wv[:, v, j, :],
                                         start=(j == 0), stop=(j == T - 1))
                    last.then_inc(sums_up, 1)

                with pe.Fori(0, n_step // 4) as q:
                    for u in range(4):
                        turn_hot(4 * q + u, u % 2)
                        edge_shifts(4 * q + u, u % 2, 4 * q + u)
                        if u:
                            sums(4 * q + (u - 1), (u - 1) % 2)
                    sums(4 * q + 3, 1)

                def turn_rows(of, n):
                    pe.wait_ge(turned5_here, n + 1)
                    for b in range(batch):
                        for k in range(KC):
                            a = (b * KC + k) * P
                            last = pe.transpose(ps[:, a // BANK, a % BANK:a % BANK + P],
                                                of[:, b, k * P:(k + 1) * P], ident[:, :])
                    last.then_inc(turned5, 1)

                def product(terms, n):
                    pe.wait_ge(banks5_free, n + 1)
                    for b in range(batch):
                        a = b * D
                        for m, (left, w, c) in enumerate(terms):
                            last = pe.matmul(ps[:, 4 + a // BANK, a % BANK:a % BANK + D],
                                             left[:, b * KC + c % KC, :], w[:, c, :],
                                             start=(m == 0), stop=(m == len(terms) - 1))
                    last.then_inc(product_up, 1)

                pe.wait_ge(sums_added, n_step + 2)
                with pe.Fori(0, n_batch) as k:
                    for v in range(1):
                        pe.wait_ge(xr_here, 16 * k + 16)
                        turn_rows(xr_slot, 3 * k)
                        pe.wait_ge(affine[0], k + 1)
                        turn_rows(y, 3 * k + 1)
                        pe.wait_ge(turned5_here, 3 * k + 3)
                        product([(y_t, w_rff, 0), (y_t, w_rff, 1)], 2 * k)
                        pe.wait_ge(z_ready, k + 1)
                        turn_rows(z, 3 * k + 2)
                        pe.wait_ge(turned5_here, 3 * k + 4)
                        product([(y_t, w_upd, 0), (y_t, w_upd, 1), (xr_t, w_upd, 2), (xr_t, w_upd, 3)],
                                2 * k + 1)

            @block.vector
            def _(vec):
                done = [0]

                def link(ins):
                    done[0] += 1
                    ins.then_inc(v_link, 1)
                    vec.wait_ge(v_link, done[0])

                vec.nop().then_inc(sums_added, 2)
                vec.nop().then_inc(v_off, 2)
                vec.nop().then_inc(va_taken, 1)
                vec.nop().then_inc(meta_used, 1)
                vec.nop().then_inc(normed[2], 1)
                vec.nop().then_inc(banks5_free, 1)
                vec.wait_ge(consts, 5)
                vec.tensor_scalar(ident[:, :], diff[:, :], 0.0, None, ALU.is_equal)
                vec.tensor_scalar(before[:, :], diff[:, :], 0.0, None, ALU.is_gt)
                vec.tensor_scalar(far_ident[:, :], diff[:, :], 0.0, -FAR, ALU.is_equal, ALU.mult)
                vec.tensor_scalar(upto[:, :], diff[:, :], 0.0, None, ALU.is_ge).then_inc(consts_made, 1)
                vec.wait_ge(src_in, 48)
                vec.tensor_copy(src_f[0:half, :, :], src_i[0:half, :, :]).then_inc(src_cast, 1)
                vec.memset(place[:, :], float(2 * n_row))
                vec.wait_ge(wk_in, 64)
                vec.tensor_tensor(fold[:, 0:KC, :], w_k[:, :, :],
                                  att[:, :].unsqueeze(1).to_broadcast([P, KC, D]), ALU.mult)
                link(vec.tensor_tensor(fold[:, KC, :], b_k[:, :], att[:, :], ALU.mult))
                for k in range(KC):
                    vec.tensor_reduce(w_va[:, k, D:VA], fold[:, k, :].rearrange("p (h c) -> p h c", h=H),
                                      AX.X, ALU.add)
                vec.tensor_reduce(b_va[:, D:VA], fold[:, KC, :].rearrange("p (h c) -> p h c", h=H),
                                  AX.X, ALU.add).then_inc(folded, 1)
                vec.wait_ge(src_turned, 1)
                for s in range(2):
                    last = vec.tensor_copy(seg_f[:, s * half:(s + 1) * half, :],
                                           ps[:, s, 0:T * half].rearrange("p (t b) -> p b t", t=T))
                link(last)
                link(vec.memset(seg_f[0:repeated // T, n_block - 1, :], float(P * (n_bin + 1))))
                link(vec.tensor_copy(seg_i[:, :], seg_f[:, :, :].rearrange("p b t -> p (b t)")))
                link(vec.tensor_scalar(bin_i[:, :], seg_i[:, :], P.bit_length() - 1, None,
                                       ALU.logical_shift_right))
                link(vec.tensor_copy(bin_h[:, :], bin_i[:, :]))
                for b in range(n_bin):
                    vec.tensor_scalar(mask[:, b, :], bin_h[:, :], float(b), None, ALU.is_equal)\
                       .then_inc(masks_made, 1)
                vec.wait_ge(totals_up, 1)
                vec.tensor_copy(tot_c[0:n_bin, :], ps[0:n_bin, 2, 128:129]).then_inc(tot_c_down, 1)
                link(vec.tensor_copy(total[:, :], ps[:, 2, 64:64 + n_bin]))
                link(vec.tensor_tensor_scan(upto_bin[:, :], total[:, :], total[:, :], 0.0, ALU.add, ALU.bypass))
                link(vec.tensor_tensor(start_at[:, :], upto_bin[:, :], total[:, :], ALU.subtract))
                link(vec.tensor_tensor(start_at[:, :], start_at[:, :], ps[:, 2, 0:n_bin], ALU.add))
                nb = n_bin
                vec.wait_ge(ends_up, 1)
                vec.tensor_scalar(ends_i[0:nb, 0:1], ps[0:nb, 3, 16:17], float(BLOCK - 1), None, ALU.add)
                vec.tensor_copy(ends_i[0:nb, 1:2], ps[0:nb, 3, 17:18])
                link(vec.tensor_copy(ends_i[0:nb, 2:3], ps[0:nb, 3, 16:17]))
                lb = BLOCK.bit_length() - 1
                vec.tensor_scalar(ends_i[0:nb, 4:6], ends_i[0:nb, 0:2], lb, None, ALU.logical_shift_right)
                link(vec.tensor_scalar(ends_i[0:nb, 6:7], ends_i[0:nb, 2:3], BLOCK - 1, None, ALU.bitwise_and))
                link(vec.tensor_copy(ends[0:nb, 0:3], ends_i[0:nb, 4:7]))
                vec.tensor_tensor(steps_c[0:nb, :], ends[0:nb, 0:1], ends[0:nb, 1:2], ALU.subtract)\
                   .then_inc(steps_down, 1)
                link(vec.tensor_scalar(mid[0:nb, :], ends[0:nb, 2:3], 1.0, None, ALU.min))
                vec.tensor_scalar(mid_w[0:nb, :], ones[0:nb, :], mid[0:nb, 0:1], None, ALU.mult)
                vec.wait_ge(steps_up, 1)
                link(vec.tensor_copy(steps_in[0:nb, :], ps[0:nb, 3, 32:33]))
                vec.tensor_scalar(passed[0:nb, :], step_no[0:nb, :], steps_in[0:nb, 0:1], None, ALU.is_ge)\
                   .then_inc(passed_down, 1)
                runs = [ps[:, 4:6, :].rearrange("p a n -> p (a n)")[:, 0:n_tile],
                        ps[:, 6:8, :].rearrange("p a n -> p (a n)")[:, 0:n_tile]]

                def put(b):
                    vec.wait_ge(runs_made, b + 1)
                    vec.wait_ge(puts_made, b)
                    vec.copy_predicated(place[:, :], mask[:, b, :], runs[b % 2]).then_inc(puts_made, 1)

                for b in range(n_bin):
                    if b >= 2:
                        vec.wait_ge(puts_made, b - 1)
                    vec.tensor_tensor_scan(runs[b % 2], mask[:, b, :], mask[:, b, :], start_at[:, b:b + 1],
                                           ALU.add, ALU.bypass).then_inc(runs_made, 1)
                    if b:
                        put(b - 1)
                put(n_bin - 1)
                vec.wait_ge(puts_made, n_bin)
                vec.tensor_scalar(place_i[:, :], place[:, :], -1.0, None, ALU.add)
                vec.wait_ge(passed_up, 1)
                vec.tensor_copy(bin_of[:, :], ps[:, 0, 0:n_step])
                link(vec.tensor_tensor(group_of[:, :], step_no[:, :], ps[:, 1, 0:n_step], ALU.subtract))
                vec.tensor_scalar(first_seg[:, :], bin_of[:, :], float(P), None, ALU.mult)
                vec.tensor_copy(bin_of_i[:, :], bin_of[:, :])
                vec.tensor_scalar(group_of_i[:, :], group_of[:, :], float(n_block - 1), 0.0, ALU.min, ALU.max)\
                   .then_inc(tables, 1)

                vec.memset(hi[:, :, :], -3.0e38)
                vec.memset(lo[:, :, :], 3.0e38).then_inc(v_score, 1)
                vec.wait_ge(filled, 16)
                vec.wait_ge(folded, 1)
                vec.wait_ge(params_in, 16 * (len(params) + len(rows_of)))

                def take_values(t, u):
                    vec.wait_ge(va_up, 2 * t + (u + 3))
                    if not isinstance(t, int):
                        vec.wait_ge(sent[u], 16 * T * t)
                    vec.tensor_tensor(row[:, u, :, 0:VA], ps[:, 4:8, 0:VA],
                                      b_va[:, :].unsqueeze(1).to_broadcast([P, T, VA]), ALU.add)\
                       .then_inc(va_taken, 1)
                    vec.wait_ge(va_taken, 2 * t + (u + 2))
                    s = row[:, u, :, D:VA]
                    vec.scalar_tensor_tensor(s, s, SLOPE, s, ALU.mult, ALU.max).then_inc(row_ready, 1)
                    vec.wait_ge(row_ready, 2 * t + (u + 1))
                    vec.wait_ge(v_score, 2 * t + (u + 1))
                    vec.tensor_tensor(hi[:, :, :], hi[:, :, :], s, ALU.max)
                    vec.tensor_tensor(lo[:, :, :], lo[:, :, :], s, ALU.min).then_inc(v_score, 1)

                for u in range(2):
                    take_values(0, u)
                with vec.Fori(1, n_block // 2) as t:
                    for u in range(2):
                        take_values(t, u)

                vec.wait_ge(v_score, n_block + 1)
                vec.tensor_reduce(ext[:, 0:H], hi[:, :, :].rearrange("p t h -> p h t"), AX.X, ALU.max)
                link(vec.tensor_reduce(ext[:, H:2 * H], lo[:, :, :].rearrange("p t h -> p h t"), AX.X, ALU.min))
                vec.tensor_scalar(ext[:, H:2 * H], ext[:, H:2 * H], -1.0, None, ALU.mult).then_inc(ext_ready, 1)
                vec.wait_ge(ext_reduced, 1)
                vec.tensor_copy(shift[:, :, :], ext_all[:, 0:H].unsqueeze(1).to_broadcast([P, n_bin + 1, H]))
                link(vec.tensor_tensor(span[:, :], ext_all[:, 0:H], ext_all[:, H:2 * H], ALU.add))
                link(vec.tensor_reduce(span1[:, :], span[:, :], AX.X, ALU.max))
                vec.tensor_scalar(wide[:, :], span1[:, :], SPAN, None, ALU.is_gt).then_inc(wide_known, 1)
                vec.wait_ge(wide_known, 1)
                far = vec.value_load(wide[0:1, 0:1], min_val=0, max_val=1)
                with vec.If(far > 0):
                    vec.memset(shift[:, :, :], FAR).then_inc(v_max, 1)
                    with vec.Fori(0, n_step) as i:
                        b = vec.value_load(bin_of_i[0:1, ds(i, 1)], min_val=0, max_val=n_bin)
                        vec.wait_ge(meta_in, 16 * i + 16)
                        vec.tensor_tensor(seg_m[:, :], meta[:, :, H],
                                          first_seg[:, ds(i, 1)].to_broadcast([P, T]), ALU.subtract)\
                           .then_inc(v_max, 1)
                        vec.wait_ge(v_max, (2 + T) * i + 2)
                        for j in range(T):
                            last = vec.tensor_scalar(outside[:, j, :], col[:, :], seg_m[:, j:j + 1], -1.0,
                                                     ALU.not_equal, ALU.mult)
                        last.then_inc(outside_made, 1)
                        for j in range(T):
                            last = vec.tensor_tensor(spread[:, :, :],
                                                     ident[:, :].unsqueeze(1).to_broadcast([P, H, P]),
                                                     meta[:, j, 0:H].unsqueeze(2).to_broadcast([P, H, P]),
                                                     ALU.mult)
                            last.then_inc(spread_made, 1)
                            vec.wait_ge(scores_up, T * i + (j + 1))
                            vec.tensor_reduce(seg_max[:, :], ps[:, 0:2, :].rearrange("p g (h e) -> p (g h) e", e=P),
                                              AX.X, ALU.max).then_inc(v_max, 1)
                            vec.wait_ge(v_max, (2 + T) * i + (3 + j))
                            last = vec.tensor_tensor(shift[:, b, :], shift[:, b, :], seg_max[:, :], ALU.max)
                        last.then_inc(v_max, 1)
                        vec.nop().then_inc(meta_used, 1)
                vec.memset(mid[:, :], 1.0).then_inc(shifts_known, 1)

                def offsets(n, u):
                    v = u % 2
                    vec.wait_ge(shift_up, n + 3)
                    vec.tensor_tensor(off[:, v, :, :], loaded[:, u, :, D:VA],
                                      ps[:, 2 + v, 0:T * H].rearrange("p (t h) -> p t h", t=T), ALU.subtract)\
                       .then_inc(v_off, 1)
                    vec.wait_ge(v_off, n + 3)
                    vec.tensor_scalar(off[:, v, :, :], off[:, v, :, :], 0.0, None, ALU.min).then_inc(off_made, 1)

                def weigh(n, u):
                    v = u % 2
                    vec.wait_ge(exp_made, n + 1)
                    vec.tensor_tensor(
                        wv[:, v, :, 0:D].rearrange("p t (h c) -> p t h c", h=H),
                        loaded[:, u, :, 0:D].rearrange("p t (h c) -> p t h c", h=H),
                        wv[:, v, :, D:VA].unsqueeze(3).to_broadcast([P, T, H, C]), ALU.mult)\
                       .then_inc(wv_made, 1)

                def add_sums(n, u, i):
                    v = u % 2
                    b = vec.value_load(bin_of_i[0:1, ds(i, 1)], min_val=0, max_val=n_bin)
                    vec.wait_ge(sums_up, n + 3)
                    vec.wait_ge(sums_added, n + 2)
                    vec.tensor_tensor(acc[:, b, :], acc[:, b, :], ps[:, 4 + v, 0:VA], ALU.add)\
                       .then_inc(sums_added, 1)

                vec.wait_ge(acc_clear, 1)
                with vec.Fori(0, n_step // 4) as q:
                    for u in range(4):
                        offsets(4 * q + u, u)
                        if u:
                            weigh(4 * q + (u - 1), u - 1)
                        if u > 1:
                            add_sums(4 * q + (u - 2), u - 2, 4 * q + (u - 2))
                    weigh(4 * q + 3, 3)
                    add_sums(4 * q + 2, 2, 4 * q + 2)
                    add_sums(4 * q + 3, 3, 4 * q + 3)

                vec.wait_ge(sums_added, n_step + 2)
                LINKS = 24
                with vec.Fori(0, n_batch) as k:
                    at_ = [0]

                    def link5(ins):
                        at_[0] += 1
                        ins.then_inc(v_link5, 1)
                        vec.wait_ge(v_link5, LINKS * k + at_[0])

                    def norm(to, of, n, done_):
                        for b in range(batch):
                            last = vec.bn_stats(stats[:, b, :], of[:, b, :])
                        link5(last)
                        vec.memset(pause[:, 1:2], 0.0)
                        for b in range(batch):
                            last = vec.bn_aggr(mv[:, b, :], stats[:, b, :])
                        last.then_inc(var_ready, 1)
                        vec.wait_ge(root_made, 3 * k + (n + 1))
                        link5(vec.reciprocal(rstd[:, :], sd[:, :]))
                        for b in range(batch):
                            last = vec.tensor_scalar(to[:, b, :], of[:, b, :], mv[:, b, 0:1], rstd[:, b:b + 1],
                                                     ALU.subtract, ALU.mult)
                        last.then_inc(done_, 1)

                    s = acc[:, ds(k * batch, batch), :]
                    link5(vec.tensor_scalar(den[:, :, :], s[:, :, D:VA], DENOM_MIN, None, ALU.max))
                    link5(vec.reciprocal(rec[:, :, :], den[:, :, :]))
                    link5(vec.tensor_tensor(y.rearrange("p b (h c) -> p b h c", h=H),
                                            s[:, :, 0:D].rearrange("p b (h c) -> p b h c", h=H),
                                            rec[:, :, :].unsqueeze(3).to_broadcast([P, batch, H, C]), ALU.mult))
                    link5(vec.tensor_tensor(y, y, att[:, :].unsqueeze(1).to_broadcast([P, batch, D]), ALU.add))
                    norm(y, y, 0, normed[0])
                    up = ps[:, 4:8, :].rearrange("p a n -> p (a n)")[:, 0:batch * D].rearrange(
                        "p (b n) -> p b n", n=D)

                    def bias_relu_add(to, bias, rest, n):
                        vec.wait_ge(product_up, 2 * k + (n + 1))
                        vec.tensor_tensor(to, up, bias[:, :].unsqueeze(1).to_broadcast([P, batch, D]), ALU.add)\
                           .then_inc(banks5_free, 1)
                        vec.wait_ge(banks5_free, 2 * k + (n + 2))
                        link5(vec.scalar_tensor_tensor(to, to, 0.0, rest, ALU.max, ALU.add))

                    bias_relu_add(z, brff, y, 0)
                    norm(z, z, 1, normed[1])
                    vec.wait_ge(res_sent, 16 * k + 16)
                    bias_relu_add(res, bupd, xr_slot, 1)
                    norm(res, res, 2, normed[2])
                    while at_[0] < LINKS:
                        at_[0] += 1
                        vec.nop().then_inc(v_link5, 1)


_INS = ["x", "src", "edge_attr_256", "L0_gnn_W_v2e", "L0_gnn_b_v2e", "L0_gnn_W_K", "L0_gnn_b_K",
        "L0_gnn_W_V", "L0_gnn_b_V", "L0_gnn_att_r", "L0_gnn_ln0_g", "L0_gnn_ln0_b", "L0_gnn_ln1_g",
        "L0_gnn_ln1_b", "L0_gnn_W_rff", "L0_gnn_b_rff", "L0_gnn_W_upd", "L0_gnn_b_upd"]


def kernel(**inputs):
    import numpy as np
    import concourse.bacc as bacc
    from concourse.bass_utils import run_bass_kernel_spmd

    nc = bacc.Bacc("TRN2", target_bir_lowering=False, num_devices=1)
    arrays, args = {}, []
    for name in _INS:
        a = np.ascontiguousarray(inputs[name])
        arrays[f"in_{name}"] = a
        args.append(nc.dram_tensor(f"in_{name}", a.shape, mybir.dt.from_np(a.dtype), kind="ExternalInput").ap())
    args.append(nc.dram_tensor("out_0", inputs["x"].shape, FP32, kind="ExternalOutput").ap())
    gnn_kernel(nc, *args)
    r = run_bass_kernel_spmd(nc, [arrays], core_ids=[0])
    return r.results[0]["out_0"]
```

```python
import concourse.bass as bass
from concourse import mybir
from concourse.bass import ds
from contextlib import ExitStack

FP32 = mybir.dt.float32
FP32R = mybir.dt.float32r
BF16 = mybir.dt.bfloat16
I16 = mybir.dt.int16
I32 = mybir.dt.int32
ALU = mybir.AluOpType
ACT = mybir.ActivationFunctionType
AX = mybir.AxisListType

P = 128
D = 256
KC = D // P
H = 8
C = D // H
EPS = 1e-5
SLOPE = 0.2
DENOM_MIN = 1e-16
SPAN = 30.0
FILL = -1e37
FAR = -float(2 ** 100)

T = 4
BLOCK = T * P
VA = D + H
ROW = VA + 1
LATE = 12544
BANK = 512


def gnn_kernel(nc, x, src, edge, W_v2e, b_v2e, W_K, b_K, W_V, b_V, att_r, ln0_g, ln0_b, ln1_g,
               ln1_b, W_rff, b_rff, W_upd, b_upd, out):
    n_seg = x.shape[0]
    n_edge = edge.shape[0]
    n_block = -(-n_edge // BLOCK)
    last_start = n_edge - BLOCK
    repeated = (n_block - 1) * BLOCK - last_start
    n_tile = n_block * T
    n_bin = -(-n_seg // P)
    half = n_block // 2
    n_step = -(-(n_block + n_bin - 2) // 4) * 4 + 1
    n_row = n_block * BLOCK
    assert n_block % 2 == 0 and half <= P and repeated % T == 0
    batch = 7
    n_batch = n_bin // batch
    assert n_batch * batch == n_bin
    short = n_seg - (n_bin - 1) * P

    rows = nc.dram_tensor("binned_rows", (n_row, ROW), FP32).ap()
    rows_g = rows.rearrange("(g p t) d -> g p (t d)", p=P, t=T)
    rows_m = rows.rearrange("(g p t) d -> g p t d", p=P, t=T)
    x_upd = nc.dram_tensor("x_update", (n_bin * P, D), FP32).ap()
    edge_b = edge[0:(n_block - 1) * BLOCK, :].rearrange("(b p t) d -> b p (t d)", p=P, t=T)
    edge_last = edge[last_start:n_edge, :].rearrange("(p t) d -> p (t d)", t=T)

    ctx = ExitStack()
    with ctx:
        def sb(name, shape, dt=FP32):
            return ctx.enter_context(nc.sbuf_tensor(name, shape, dt))

        def sem(name):
            return ctx.enter_context(nc.semaphore(name))

        w_in = [sb(f"w_in{n}", [P, KC, D], FP32R) for n in range(2)]
        w_va = [sb(f"w_va{n}", [P, KC, VA], FP32R) for n in range(2)]
        w_rff = sb("w_rff", [P, KC, D])
        w_upd = sb("w_upd", [P, 2 * KC, D])
        cols_in = sb("cols_in", [5 * KC, P])
        cols = sb("cols", [P, 5, KC])
        att = sb("att", [P, D])
        b_va = sb("b_va", [P, VA])
        g0, c0 = sb("g0", [P, D]), sb("c0", [P, D])
        bias_row = sb("bias_row", [1, 2, D])
        col = sb("col", [P, P])
        diff = sb("diff", [P, P])
        ident = sb("ident", [P, P])
        before = sb("before", [P, P])
        upto = sb("upto", [P, P])
        ones = sb("ones", [P, P])
        eps = sb("eps", [P, 1])
        step_no = sb("step_no", [P, n_step])
        far_ident = sb("far_ident", [P, P], BF16)
        seg_f = sb("seg_f", [P, n_block, T])
        bin_h = sb("bin_h", [P, n_tile], BF16)
        sums_w = (n_bin + 1) * VA
        early = sb("early", [P, n_bin * n_tile // 2])
        mask = early[:, :].bitcast(I16).rearrange("p (b t) -> p b t", b=n_bin)
        acc = early[:, 0:sums_w].rearrange("p (b v) -> p b v", v=VA)
        late = sb("late", [P, LATE])
        lows = sb("lows", [P, 16 * BLOCK], FP32R)

        def cutter(region, start, end):
            at_ = [start]

            def take(*shape):
                n = 1
                for k in shape:
                    n *= k
                at_[0] += n
                assert at_[0] <= end
                v = region[:, at_[0] - n:at_[0]]
                names = "abc"[:len(shape)]
                if len(shape) == 1:
                    return v
                return v.rearrange(f"p ({' '.join(names)}) -> p {' '.join(names)}",
                                   **{m: k for m, k in zip(names, shape)})
            return take

        take = cutter(late, 0, LATE)
        src_i = take(2, BLOCK).bitcast(I32)
        src_f = take(2, BLOCK)
        seg_i = take(n_tile).bitcast(I32)
        bin_i = take(n_tile).bitcast(I32)
        place = take(n_tile)
        fold = take(KC + 1, D)
        b_k = take(D)
        x_in = take(2, D)
        x_turned = take(2, KC, P)
        x_made = take(2, D)
        raw_in, raw_k, raw_va = take(KC, D), take(KC, D), take(KC, VA)
        x_f = take(KC, BLOCK)
        take = cutter(early, sums_w, n_bin * n_tile // 2)
        e_in = take(2, T * D)
        row = take(2, T, ROW)
        take = cutter(lows, 0, 16 * BLOCK)
        e_t = [take(2, KC, BLOCK) for n in range(2)]
        x_t = [take(2, KC, BLOCK) for n in range(2)]
        take = cutter(early, sums_w, n_bin * n_tile // 2)
        loaded = take(4, T, ROW)
        take = cutter(late, 0, LATE)
        hot = take(2, T, P)
        hot_t = take(2, T, P)
        wv = take(2, T, VA)
        spread = take(H, P)
        take = cutter(early, sums_w, n_bin * n_tile // 2)
        xr, xu, res = take(batch, D), take(batch, D), take(batch, D)
        take = cutter(late, 0, LATE)
        y, y_res, z = take(batch, D), take(batch, D), take(batch, D)
        up1, up2 = take(batch, D), take(batch, D)
        y_t, z_t = take(batch * KC, P), take(batch * KC, P)
        spare = sb("spare", [P, 2, n_tile], BF16)
        count = sb("count", [P, n_bin])
        total = sb("total", [P, n_bin])
        upto_bin = sb("upto_bin", [P, n_bin])
        start_at = sb("start_at", [P, n_bin])
        place_i = sb("place_i", [P, n_tile], I32)
        tot_c = sb("tot_c", [P, 1])
        ends = sb("ends", [P, 4])
        ends_i = sb("ends_i", [P, 8], I32)
        mid = sb("mid", [P, 1])
        steps_c = sb("steps_c", [P, 1])
        steps_in = sb("steps_in", [P, 1])
        mid_w = sb("mid_w", [P, P])
        passed = sb("passed", [P, n_step])
        bin_of = sb("bin_of", [P, n_step])
        first_seg = sb("first_seg", [P, n_step])
        group_of = sb("group_of", [P, n_step])
        bin_of_i = sb("bin_of_i", [P, n_step], I32)
        group_of_i = sb("group_of_i", [P, n_step], I32)
        den = sb("den", [P, batch, H])
        rec = sb("rec", [P, batch, H])
        stats = sb("stats", [P, batch, 6])
        mv = sb("mv", [P, batch, 2])
        sd = sb("sd", [P, batch])
        rstd = sb("rstd", [P, batch])
        at = sb("at", [P, 2, T], I32)
        fill = late[:, LATE - T * ROW:LATE]
        hi = sb("hi", [P, T, H])
        lo = sb("lo", [P, T, H])
        ext = sb("ext", [P, 2 * H])
        ext_all = sb("ext_all", [P, 2 * H])
        span = sb("span", [P, H])
        span1 = sb("span1", [P, 1])
        wide = sb("wide", [P, 1], I32)
        shift = sb("shift", [P, n_bin + 1, H])
        meta = sb("meta", [P, T, H + 1])
        seg_m = sb("seg_m", [P, T])
        outside = sb("outside", [P, T, P], BF16)
        seg_max = sb("seg_max", [P, H])
        pause = sb("pause", [P, 2])
        from_seg = sb("from_seg", [P, 2])
        off = sb("off", [P, 2, T, H])

        ps = ctx.enter_context(nc.psum_tensor("ps", [P, 8, BANK], FP32))

        params_in = sem("params_in")
        wk_in = sem("wk_in")
        src_in = sem("src_in")
        consts = sem("consts")
        folded = sem("folded")
        v_link = sem("v_link")
        src_cast = sem("src_cast")
        src_turned = sem("src_turned")
        masks_made = sem("masks_made")
        counted = sem("counted")
        totals_up = sem("totals_up")
        tot_c_up, tot_c_down = sem("tot_c_up"), sem("tot_c_down")
        ends_up = sem("ends_up")
        steps_down, steps_up = sem("steps_down"), sem("steps_up")
        passed_down, passed_up = sem("passed_down"), sem("passed_up")
        tables = sem("tables")
        filled, fill_set = sem("filled"), sem("fill_set")
        e_here = [sem("e_here0"), sem("e_here1")]
        e_turned, e_high, e_low = sem("e_turned"), sem("e_high"), sem("e_low")
        x_up, x_high, x_whole, x_low = sem("x_up"), sem("x_high"), sem("x_whole"), sem("x_low")
        xt_here, xt_turned, xt_down = [sem("xt_here0"), sem("xt_here1")], sem("xt_turned"), sem("xt_down")
        xt_up, xt_made = sem("xt_up"), sem("xt_made")
        xt_stored = [sem("xt_stored0"), sem("xt_stored1")]
        va_up, va_taken = sem("va_up"), sem("va_taken")
        row_ready = sem("row_ready")
        v_score = sem("v_score")
        row_meta = sem("row_meta")
        sent = [sem("sent0"), sem("sent1")]
        ext_ready, ext_reduced, wide_known = sem("ext_ready"), sem("ext_reduced"), sem("wide_known")
        meta_in, meta_used = sem("meta_in"), sem("meta_used")
        v_max, outside_made, spread_made = sem("v_max"), sem("outside_made"), sem("spread_made")
        scores_up = sem("scores_up")
        shifts_known = sem("shifts_known")
        loaded_in = [sem(f"loaded_in{k}") for k in range(4)]
        from_made, hot_a, hot_b = sem("from_made"), sem("hot_a"), sem("hot_b")
        hot_turned, hot_t_here = sem("hot_turned"), sem("hot_t_here")
        shift_up = sem("shift_up")
        v_off, off_made, exp_made, wv_made = sem("v_off"), sem("off_made"), sem("exp_made"), sem("wv_made")
        sums_up, sums_added = sem("sums_up"), sem("sums_added")

        acc_clear, steps_made, split = sem("acc_clear"), sem("steps_made"), sem("split")
        z_read = sem("z_read")
        cols_turned, cols_here = sem("cols_turned"), sem("cols_here")
        consts_made, runs_made, puts_made = sem("consts_made"), sem("runs_made"), sem("puts_made")
        normed = [sem(f"normed{n}") for n in range(3)]
        v_link5, y_res_made, p_link = sem("v_link5"), sem("y_res_made"), sem("p_link")
        var_ready, root_made = sem("var_ready"), sem("root_made")
        y_turned, z_turned, y_t_here, z_t_here = (sem("y_turned"), sem("z_turned"), sem("y_t_here"),
                                                  sem("z_t_here"))
        product1, product2, up1_here, up2_here = (sem("product1"), sem("product2"), sem("up1_here"),
                                                  sem("up2_here"))
        updated, res_made = sem("updated"), sem("res_made")
        xr_here, xu_here, res_sent = sem("xr_here"), sem("xu_here"), sem("res_sent")

        params = [
            (raw_in[:, :, :], W_v2e.rearrange("(k p) n -> p k n", p=P)),
            (raw_va[:, :, 0:D], W_V.rearrange("(k p) n -> p k n", p=P)),
            (w_rff[:, :, :], W_rff.rearrange("(k p) n -> p k n", p=P)),
            (w_upd[:, :, :], W_upd.rearrange("(k p) n -> p k n", p=P)),
            (bias_row[:, 0, :], b_rff.rearrange("(o n) -> o n", o=1)),
            (bias_row[:, 1, :], b_upd.rearrange("(o n) -> o n", o=1)),
        ]
        rows_of = [(b_va[:, 0:D], b_V), (g0[:, :], ln0_g), (c0[:, :], ln0_b)]

        def every(v):
            return v.rearrange("(o n) -> o n", o=1).broadcast_to([P, v.shape[0]])

        with nc.Block() as block:

            @block.sync
            def _(sp):
                sp.dma_start(src_i[0:half, 0, :],
                             src[0:half * BLOCK].rearrange("(b n) -> b n", n=BLOCK)).then_inc(src_in, 16)
                sp.dma_start(src_i[0:half - 1, 1, :],
                             src[half * BLOCK:(n_block - 1) * BLOCK].rearrange("(b n) -> b n", n=BLOCK))\
                  .then_inc(src_in, 16)
                sp.dma_start(src_i[half - 1:half, 1, :],
                             src[last_start:n_edge].rearrange("(b n) -> b n", n=BLOCK)).then_inc(src_in, 16)
                for dst, of in params:
                    sp.dma_start(dst, of).then_inc(params_in, 16)
                for dst, of in rows_of:
                    sp.dma_start(dst, every(of)).then_inc(params_in, 16)
                x_b = x[0:(n_bin - 1) * P, :].rearrange("(b p) d -> b p d", p=P)
                xu_b = x_upd.rearrange("(b p) d -> b p d", p=P)

                def load_x(of, part, u):
                    sp.dma_start(x_in[part, u, :], of).then_inc(xt_here[u], 16)

                def store_x(b, u, n):
                    sp.wait_ge(xt_made, n + 2)
                    sp.dma_start(xu_b[b], x_made[:, u, :]).then_inc(xt_stored[u], 16)

                everyone = slice(0, P)
                load_x(x_b[0], everyone, 0)
                load_x(x_b[1], everyone, 1)
                with sp.Fori(0, (n_bin - 3) // 2) as t:
                    for u in range(2):
                        store_x(2 * t + u, u, 2 * t + u)
                        load_x(x_b[2 * t + (u + 2)], everyone, u)
                store_x(n_bin - 3, 0, n_bin - 3)
                load_x(x[(n_bin - 1) * P:n_seg, :], slice(0, short), 0)
                store_x(n_bin - 2, 1, n_bin - 2)
                store_x(n_bin - 1, 0, n_bin - 1)
                sp.wait_ge(tables, 1)
                def load_block(of, u):
                    sp.dma_start(e_in[:, u, :], of).then_inc(e_here[u], 16)
                load_block(edge_b[0], 0)
                load_block(edge_b[1], 1)
                with sp.Fori(1, n_block // 2 - 1) as t:
                    for u in range(2):
                        sp.wait_ge(e_turned, 2 * t + (u - 1))
                        load_block(edge_b[2 * t + u], u)
                sp.wait_ge(e_turned, n_block - 3)
                load_block(edge_b[n_block - 2], 0)
                sp.wait_ge(e_turned, n_block - 2)
                load_block(edge_last, 1)
                for u in range(2):
                    sp.wait_ge(sent[u], 16 * T * (n_block // 2))
                sp.wait_ge(filled, 16)
                sp.wait_ge(tables, 1)
                sp.wait_ge(wide_known, 1)
                far = sp.value_load(wide[0:1, 0:1], min_val=0, max_val=1)
                with sp.If(far > 0):
                    with sp.Fori(0, n_step) as i:
                        sp.wait_ge(meta_used, i + 1)
                        g = sp.value_load(group_of_i[0:1, ds(i, 1)], min_val=0, max_val=n_block - 1)
                        sp.dma_start(meta[:, :, :], rows_m[g][:, :, D:ROW]).then_inc(meta_in, 16)
                def load_step(n, u):
                    g = sp.value_load(group_of_i[0:1, ds(n, 1)], min_val=0, max_val=n_block - 1)
                    sp.dma_start(loaded[:, u, :, :].rearrange("p t d -> p (t d)"), rows_g[g])\
                      .then_inc(loaded_in[u], 16)
                for n in range(4):
                    load_step(n, n)
                sp.wait_ge(wv_made, 1)
                sp.wait_ge(hot_b, 1)
                load_step(4, 0)
                with sp.Fori(0, (n_step - 5) // 4) as q:
                    for u in range(4):
                        sp.wait_ge(wv_made, 4 * q + (u + 2))
                        sp.wait_ge(hot_b, 4 * q + (u + 2))
                        load_step(4 * q + (u + 5), (u + 1) % 4)
                full = (n_bin - 1) * P

                def batch_rows(t, k):
                    return t[0:(t.shape[0] // P) * P, :].rearrange("(b p) d -> p b d", p=P)\
                        [:, ds(k * batch, batch), :]

                def store_batch(k, n):
                    sp.wait_ge(normed[2], n + 1)
                    sp.dma_start(batch_rows(out, k), res).then_inc(res_sent, 16)

                sp.wait_ge(sums_added, n_step + 2)
                for u in range(2):
                    sp.wait_ge(xt_stored[u], 16 * ((n_bin + 1 - u) // 2))
                sp.dma_start(xr, batch_rows(x, 0)).then_inc(xr_here, 16)
                sp.dma_start(xu, batch_rows(x_upd, 0)).then_inc(xu_here, 16)
                with sp.Fori(0, n_batch - 2) as k:
                    sp.wait_ge(res_made, k + 1)
                    sp.dma_start(xr, batch_rows(x, k + 1)).then_inc(xr_here, 16)
                    sp.dma_start(xu, batch_rows(x_upd, k + 1)).then_inc(xu_here, 16)
                    store_batch(k, k)
                sp.wait_ge(res_made, n_batch - 1)
                k = n_batch - 1
                sp.dma_start(xu, batch_rows(x_upd, k)).then_inc(xu_here, 16)
                sp.dma_start(xr[:, 0:batch - 1, :],
                             x[k * batch * P:full, :].rearrange("(b p) d -> p b d", p=P)).then_inc(xr_here, 16)
                sp.dma_start(xr[0:short, batch - 1, :], x[full:n_seg, :]).then_inc(xr_here, 16)
                store_batch(n_batch - 2, n_batch - 2)
                sp.wait_ge(normed[2], n_batch)
                sp.dma_start(out[k * batch * P:full, :].rearrange("(b p) d -> p b d", p=P),
                             res[:, 0:batch - 1, :]).then_inc(res_sent, 16)
                sp.dma_start(out[full:n_seg, :], res[0:short, batch - 1, :]).then_inc(res_sent, 16)
                sp.wait_ge(res_sent, 16 * (n_batch + 1))

            @block.gpsimd
            def _(pool):
                pool.iota(col[:, :], [[1, P]], base=0, channel_multiplier=0,
                          allow_small_or_imprecise_dtypes=True).then_inc(consts, 1)
                pool.iota(diff[:, :], [[1, P]], base=0, channel_multiplier=-1,
                          allow_small_or_imprecise_dtypes=True).then_inc(consts, 1)
                pool.iota(step_no[:, :], [[1, n_step]], base=0, channel_multiplier=0,
                          allow_small_or_imprecise_dtypes=True).then_inc(consts, 1)
                pool.memset(ones[:, :], 1.0).then_inc(consts, 1)
                pool.memset(eps[:, :], EPS).then_inc(consts, 1)
                pool.memset(fill, FILL).then_inc(fill_set, 1)
                pool.wait_ge(fill_set, 1)
                pool.dma_start(rows[n_edge:n_row, :].rearrange("(p t) d -> p (t d)", t=T),
                               fill[0:(n_row - n_edge) // T, :]).then_inc(filled, 16)
                pool.wait_ge(filled, 16)
                pool.wait_ge(tables, 1)
                limit, bound = pool.alloc_register("limit"), pool.alloc_register("bound")
                pool.reg_mov(limit, n_row - 2)
                pool.reg_mov(bound, n_row - 1)

                def send(t, u):
                    if not isinstance(t, int):
                        pool.wait_ge(sent[u], 16 * T * t)
                    pool.tensor_copy(at[:, u, :], place_i[:, ds((2 * t + u) * T, T)]).then_inc(row_meta, 1)
                    pool.tensor_copy(row[:, u, :, VA:ROW],
                                     seg_f[:, ds(2 * t + u, 1), :].rearrange("p o t -> p t o"))\
                        .then_inc(row_meta, 1)
                    pool.wait_ge(row_ready, 2 * t + u + 1)
                    pool.wait_ge(row_meta, 4 * t + 2 * u + 2)
                    pool.reg_add(bound, limit, 1)
                    for j in range(T):
                        pool.indirect_dma_start(
                            rows, bass.IndirectOffsetOnAxis(ap=at[:, u, j:j + 1], axis=0),
                            row[:, u, j, :], None, bounds_check=bound, oob_is_err=False)\
                            .then_inc(sent[u], 16)

                for u in range(2):
                    send(0, u)
                with pool.Fori(1, n_block // 2) as t:
                    for u in range(2):
                        send(t, u)
                pool.wait_ge(ext_ready, 1)
                pool.partition_all_reduce(ext_all[:, :], ext[:, :], P, bass.bass_isa.ReduceOp.max)\
                    .then_inc(ext_reduced, 1)
                pool.memset(acc[:, :, :], 0.0).then_inc(acc_clear, 1)
                def hot_step(n, here, u):
                    v = u % 2
                    pool.wait_ge(sums_up, n + 1)
                    pool.tensor_copy(from_seg[:, v:v + 1], first_seg[:, ds(n, 1)]).then_inc(from_made, 1)
                    pool.wait_ge(loaded_in[u], here)
                    pool.wait_ge(from_made, n + 1)
                    pool.tensor_tensor(pause[:, 0:1], eps[:, :], eps[:, :], ALU.add)
                    for j in range(T // 2, T):
                        last = pool.tensor_scalar(hot[:, v, j, :], col[:, :], from_seg[:, v:v + 1],
                                                  loaded[:, u, j, VA:ROW], ALU.add, ALU.is_equal)
                    last.then_inc(hot_b, 1)

                hot_step(0, 16, 0)
                with pool.Fori(0, (n_step - 1) // 4) as q:
                    for u in range(4):
                        hot_step(4 * q + (u + 1), 16 * q + (32 if u == 3 else 16), (u + 1) % 4)

                pool.wait_ge(sums_added, n_step + 2)

                def affine(n):
                    pool.wait_ge(normed[0], n + 1)
                    pool.wait_ge(z_read, n + 1)
                    pool.tensor_tensor(y_res, y, g0[:, :].unsqueeze(1).to_broadcast([P, batch, D]),
                                       ALU.mult).then_inc(p_link, 1)
                    pool.wait_ge(p_link, n + 1)
                    pool.tensor_tensor(y_res, y_res, c0[:, :].unsqueeze(1).to_broadcast([P, batch, D]),
                                       ALU.add).then_inc(y_res_made, 1)

                def add_update(n):
                    pool.wait_ge(up2_here, n + 2)
                    pool.wait_ge(xu_here, 16 * n + 16)
                    pool.tensor_tensor(up2, up2, xu, ALU.add).then_inc(updated, 1)

                affine(0)
                with pool.Fori(1, n_batch) as k:
                    affine(k)
                    add_update(k - 1)
                add_update(n_batch - 1)

            @block.scalar
            def _(act):
                act.nop().then_inc(hot_t_here, 1)
                act.nop().then_inc(y_t_here, 1)
                act.nop().then_inc(z_t_here, 1)
                act.nop().then_inc(up1_here, 1)
                act.nop().then_inc(up2_here, 1)
                act.nop().then_inc(xt_down, 1)
                act.nop().then_inc(xt_made, 1)
                act.dma_start(raw_k[:, :, :], W_K.rearrange("(k p) n -> p k n", p=P)).then_inc(wk_in, 16)
                act.dma_start(att[:, :], every(att_r.rearrange("a h c -> (a h c)"))).then_inc(wk_in, 16)
                act.dma_start(b_k, every(b_K)).then_inc(wk_in, 16)
                for n, v in enumerate((b_v2e, ln0_g, ln0_b, ln1_g, ln1_b)):
                    act.dma_start(cols_in[n * KC:(n + 1) * KC, :], v.rearrange("(k p) -> k p", p=P))\
                       .then_inc(wk_in, 16)
                act.wait_ge(cols_turned, 1)
                act.activation(cols[:, :, :], ps[:, 3, 0:5 * KC].rearrange("p (n k) -> p n k", k=KC),
                               ACT.Copy).then_inc(cols_here, 1)
                for b in range(n_bin):
                    act.wait_ge(masks_made, b + 1)
                    if b >= 2:
                        act.wait_ge(counted, b - 1)
                    act.activation(spare[:, b % 2, :], mask[:, b, :], ACT.Copy, accum_out=count[:, b:b + 1])\
                       .then_inc(counted, 1)
                act.wait_ge(cols_here, 1)

                def take_x(n, u):
                    act.wait_ge(xt_turned, n + 1)
                    act.activation(x_turned[:, u, :, :], ps[:, u, 0:KC * P].rearrange("p (k e) -> p k e", k=KC),
                                   ACT.Copy).then_inc(xt_down, 1)

                def take_update(n, u):
                    act.wait_ge(xt_up, n + 1)
                    act.activation(x_made[:, u, :], ps[:, 2 + u, 0:D], ACT.Copy).then_inc(xt_made, 1)

                take_x(0, 0)
                take_x(1, 1)
                take_update(0, 0)
                take_x(2, 0)
                take_update(1, 1)
                with act.Fori(1, (n_bin - 1) // 2) as t:
                    for u in range(2):
                        act.wait_ge(xt_stored[u], 16 * t)
                        take_x(2 * t + (u + 1), 1 - u)
                        take_update(2 * t + u, u)
                act.wait_ge(xt_stored[0], 16 * ((n_bin - 1) // 2))
                take_update(n_bin - 1, 0)

                def edges_high(n, u):
                    act.wait_ge(e_turned, n + 1)
                    act.wait_ge(x_up, n + 1)
                    for k in range(KC):
                        last = act.activation(e_t[0][:, u, k, :], ps[:, k, :], ACT.Copy)
                    last.then_inc(e_high, 1)

                def hidden_high(n, u):
                    act.wait_ge(x_up, n + 3)
                    act.wait_ge(va_up, n + 1)
                    for k in range(KC):
                        last = act.activation(x_t[0][:, u, k, :], ps[:, 2 + k, :], ACT.Relu,
                                              bias=cols[:, 0, k:k + 1])
                    last.then_inc(x_high, 1)
                    act.wait_ge(x_low, n + 1)
                    for k in range(KC):
                        last = act.activation(x_f[:, k, :], ps[:, 2 + k, :], ACT.Relu,
                                              bias=cols[:, 0, k:k + 1])
                    last.then_inc(x_whole, 1)

                edges_high(0, 0)
                with act.Fori(0, n_block // 2 - 1) as t:
                    for u in range(2):
                        edges_high(2 * t + (u + 1), 1 - u)
                        hidden_high(2 * t + u, u)
                edges_high(n_block - 1, 1)
                hidden_high(n_block - 2, 0)
                hidden_high(n_block - 1, 1)

                def exps(n, v):
                    act.wait_ge(off_made, n + 1)
                    act.wait_ge(sums_up, n + 1)
                    act.activation(wv[:, v, :, D:VA], off[:, v, :, :], ACT.Exp).then_inc(exp_made, 1)

                def turned_hot(n, v):
                    act.wait_ge(hot_turned, n + 1)
                    act.wait_ge(shift_up, n + 1)
                    act.activation(hot_t[:, v, :, :], ps[:, v, :].rearrange("p (t e) -> p t e", t=T),
                                   ACT.Copy).then_inc(hot_t_here, 1)

                act.wait_ge(wide_known, 1)
                far = act.value_load(wide[0:1, 0:1], min_val=0, max_val=1)
                with act.If(far > 0):
                    turned_hot(0, 0)
                    exps(0, 0)
                    with act.Fori(0, (n_step - 1) // 2) as q:
                        for u in range(2):
                            turned_hot(2 * q + (u + 1), 1 - u)
                            exps(2 * q + (u + 1), 1 - u)
                with act.Else():
                    exps(0, 0)
                    with act.Fori(0, (n_step - 1) // 2) as q:
                        for u in range(2):
                            exps(2 * q + (u + 1), 1 - u)

                def root(n):
                    act.wait_ge(var_ready, n + 1)
                    act.activation(sd[:, :], mv[:, :, 1], ACT.Sqrt, bias=eps[:, 0:1]).then_inc(root_made, 1)

                def take_turned(to, turned, here, n, func, c):
                    act.wait_ge(turned, n + 1)
                    for k in range(KC):
                        of = ps[:, 0:4, :].rearrange("p a n -> p (a n)")[:, 0:batch * KC * P]\
                            .rearrange("p (b k n) -> p k b n", k=KC, n=P)[:, k, :, :]
                        last = act.activation(to.rearrange("p (b k) n -> p k b n", k=KC)[:, k, :, :], of, func,
                                              bias=cols[:, c + 1, k:k + 1], scale=cols[:, c, k:k + 1])
                    last.then_inc(here, 1)

                def take_product(to, up, here, n):
                    act.wait_ge(up, n + 1)
                    act.activation(to, ps[:, 4:8, :].rearrange("p a n -> p (a n)")[:, 0:batch * D]
                                   .rearrange("p (b n) -> p b n", n=D), ACT.Copy).then_inc(here, 1)

                def first(n):
                    take_turned(y_t, y_turned, y_t_here, n, ACT.Identity, 1)
                    act.wait_ge(z_read, n + 1)
                    take_product(up1, product1, up1_here, n)

                def second(n):
                    take_turned(z_t, z_turned, z_t_here, n, ACT.Relu, 3)
                    if not isinstance(n, int) or n:
                        act.wait_ge(res_made, n)
                    take_product(up2, product2, up2_here, n)

                root(0)
                first(0)
                root(1)
                root(2)
                first(1)
                second(0)
                with act.Fori(2, n_batch) as k:
                    root(3 * k - 3)
                    root(3 * k - 2)
                    root(3 * k - 1)
                    first(k)
                    second(k - 1)
                root(3 * n_batch - 3)
                root(3 * n_batch - 2)
                second(n_batch - 1)
                root(3 * n_batch - 1)

            @block.tensor
            def _(pe):
                pe.nop().then_inc(x_up, 2)
                pe.nop().then_inc(va_up, 2)
                pe.nop().then_inc(sums_up, 2)
                pe.nop().then_inc(shift_up, 2)
                pe.wait_ge(consts_made, 1)
                pe.wait_ge(src_cast, 1)
                for s in range(2):
                    for j in range(T):
                        last = pe.transpose(
                            ps[:, s, j * half:(j + 1) * half],
                            src_f[0:half, s, :].rearrange("b (p t) -> b t p", t=T)[:, j, :],
                            ident[0:half, 0:half])
                last.then_inc(src_turned, 1)
                pe.wait_ge(wk_in, 128)
                pe.transpose(ps[:, 3, 0:5 * KC], cols_in[:, :], ident[0:5 * KC, 0:5 * KC])\
                  .then_inc(cols_turned, 1)
                pe.wait_ge(counted, n_bin)
                pe.wait_ge(cols_here, 1)
                pe.matmul(ps[:, 2, 0:n_bin], before[:, :], count[:, :], start=True, stop=True)
                pe.matmul(ps[:, 2, 64:64 + n_bin], ones[:, :], count[:, :], start=True, stop=True)
                pe.matmul(ps[0:n_bin, 2, 128:129], count[:, :], ones[:, 0:1], start=True, stop=True)\
                  .then_inc(totals_up, 1)
                nb = n_bin
                pe.wait_ge(tot_c_down, 1)
                pe.matmul(ps[0:nb, 3, 16:17], upto[0:nb, 0:nb], tot_c[0:nb, :], start=True, stop=True)
                pe.matmul(ps[0:nb, 3, 17:18], before[0:nb, 0:nb], tot_c[0:nb, :], start=True, stop=True)\
                  .then_inc(ends_up, 1)
                pe.wait_ge(steps_down, 1)
                pe.matmul(ps[0:nb, 3, 32:33], upto[0:nb, 0:nb], steps_c[0:nb, :], start=True, stop=True)\
                  .then_inc(steps_up, 1)
                pe.wait_ge(passed_down, 1)
                pe.matmul(ps[:, 0, 0:n_step], ones[0:nb, :], passed[0:nb, :], start=True, stop=True)
                pe.matmul(ps[:, 1, 0:n_step], mid_w[0:nb, :], passed[0:nb, :], start=True, stop=True)\
                  .then_inc(passed_up, 1)
                pe.wait_ge(steps_made, 1)
                pe.wait_ge(params_in, 16 * (len(params) + len(rows_of)))

                def turn_x(u, here, n):
                    pe.wait_ge(xt_here[u], here)
                    pe.wait_ge(xt_down, n)
                    for k in range(KC):
                        last = pe.transpose(ps[:, u, k * P:(k + 1) * P], x_in[:, u, k * P:(k + 1) * P],
                                            ident[:, :])
                    last.then_inc(xt_turned, 1)

                def update_x(u, n):
                    pe.wait_ge(xt_down, n + 2)
                    pe.wait_ge(xt_made, n + 1)
                    for k in range(KC):
                        pe.matmul(ps[:, 2 + u, 0:D], x_turned[:, u, k, :], w_upd[:, KC + k, :],
                                  start=(k == 0), stop=False)
                    pe.matmul(ps[:, 2 + u, 0:D], ones[0:1, :], bias_row[:, 1, :], start=False, stop=True)\
                      .then_inc(xt_up, 1)

                turn_x(0, 16, 0)
                with pe.Fori(0, (n_bin - 1) // 2) as t:
                    for u in range(2):
                        turn_x(1 - u, 16 * t + (16 if u == 0 else 32), 2 * t + (u + 1))
                        update_x(u, 2 * t + u)
                update_x(0, n_bin - 1)

                pe.wait_ge(tables, 1)
                pe.wait_ge(xt_made, n_bin + 1)
                pe.wait_ge(split, 1)

                def turn(u, here, n):
                    pe.wait_ge(e_here[u], here)
                    pe.wait_ge(e_low, n)
                    for k in range(KC):
                        for j in range(T):
                            at_ = j * D + k * P
                            last = pe.transpose(ps[:, k, j * P:(j + 1) * P], e_in[:, u, at_:at_ + P],
                                                ident[:, :])
                    last.then_inc(e_turned, 1)

                PARTS = [(0, 0), (0, 1), (1, 0)]

                def hidden(u, n):
                    pe.wait_ge(e_low, n + 1)
                    pe.wait_ge(x_whole, n)
                    for m in range(KC):
                        for k in range(KC):
                            for a, b in PARTS:
                                last = pe.matmul(ps[:, 2 + m, :], w_in[b][:, k, m * P:(m + 1) * P],
                                                 e_t[a][:, u, k, :], start=(k == 0 and a + b == 0),
                                                 stop=(k == KC - 1 and a == 1))
                    last.then_inc(x_up, 1)

                def values(u, n):
                    pe.wait_ge(x_low, n + 2)
                    pe.wait_ge(va_taken, n + 1)
                    for j in range(T):
                        for k in range(KC):
                            for a, b in PARTS:
                                last = pe.matmul(ps[:, 4 + j, 0:VA], x_t[a][:, u, k, j * P:(j + 1) * P],
                                                 w_va[b][:, k, :], start=(k == 0 and a + b == 0),
                                                 stop=(k == KC - 1 and a == 1))
                    last.then_inc(va_up, 1)

                turn(0, 16, 0)
                turn(1, 16, 1)
                hidden(0, 0)
                with pe.Fori(0, n_block // 2 - 1) as t:
                    for u in range(2):
                        turn(u, 16 * t + 32, 2 * t + (u + 2))
                        hidden(1 - u, 2 * t + (u + 1))
                        values(u, 2 * t + u)
                hidden(1, n_block - 1)
                values(0, n_block - 2)
                values(1, n_block - 1)

                def turn_hot(n, v):
                    pe.wait_ge(hot_a, n + 1)
                    pe.wait_ge(hot_b, n + 1)
                    pe.wait_ge(hot_t_here, n + 1)
                    for j in range(T):
                        last = pe.transpose(ps[:, v, j * P:(j + 1) * P], hot[:, v, j, :], ident[:, :])
                    last.then_inc(hot_turned, 1)

                def edge_shifts(n, v):
                    b = pe.value_load(bin_of_i[0:1, ds(n, 1)], min_val=0, max_val=n_bin)
                    pe.wait_ge(hot_t_here, n + 2)
                    pe.wait_ge(v_off, n + 1)
                    for j in range(T):
                        last = pe.matmul(ps[:, 2 + v, j * H:(j + 1) * H], hot_t[:, v, j, :], shift[:, b, :],
                                         start=True, stop=True)
                    last.then_inc(shift_up, 1)

                def sums(n, v):
                    pe.wait_ge(hot_a, n + 1)
                    pe.wait_ge(hot_b, n + 1)
                    pe.wait_ge(wv_made, n + 1)
                    pe.wait_ge(sums_added, n + 1)
                    for j in range(T):
                        last = pe.matmul(ps[:, 4 + v, 0:VA], hot[:, v, j, :], wv[:, v, j, :],
                                         start=(j == 0), stop=(j == T - 1))
                    last.then_inc(sums_up, 1)

                pe.wait_ge(wide_known, 1)
                far = pe.value_load(wide[0:1, 0:1], min_val=0, max_val=1)
                with pe.If(far > 0):
                    with pe.Fori(0, n_step) as i:
                        for j in range(T):
                            pe.wait_ge(outside_made, i + 1)
                            pe.wait_ge(spread_made, T * i + (j + 1))
                            for g in range(2):
                                pe.matmul(ps[:, g, :], outside[:, j, :],
                                          far_ident[:, :].unsqueeze(1).to_broadcast([P, H // 2, P]),
                                          start=True, stop=False)
                                last = pe.matmul(ps[:, g, :], ones[:, :],
                                                 spread[:, g * H // 2:(g + 1) * H // 2, :],
                                                 start=False, stop=True)
                            last.then_inc(scores_up, 1)
                    pe.wait_ge(shifts_known, 1)
                    turn_hot(0, 0)
                    edge_shifts(0, 0)
                    sums(0, 0)
                    with pe.Fori(0, (n_step - 1) // 2) as q:
                        for u in range(2):
                            turn_hot(2 * q + (u + 1), 1 - u)
                            edge_shifts(2 * q + (u + 1), 1 - u)
                            sums(2 * q + (u + 1), 1 - u)
                with pe.Else():
                    sums(0, 0)
                    with pe.Fori(0, (n_step - 1) // 2) as q:
                        for u in range(2):
                            sums(2 * q + (u + 1), 1 - u)

                def turn_rows(of, ready, n, turned):
                    pe.wait_ge(ready, n + 1)
                    for b in range(batch):
                        for k in range(KC):
                            a = (b * KC + k) * P
                            last = pe.transpose(ps[:, a // BANK, a % BANK:a % BANK + P],
                                                of[:, b, k * P:(k + 1) * P], ident[:, :])
                    last.then_inc(turned, 1)

                def product(left, w, n, here, bias, up):
                    pe.wait_ge(here, n + 2)
                    for b in range(batch):
                        a = b * D
                        to = ps[:, 4 + a // BANK, a % BANK:a % BANK + D]
                        for k in range(KC):
                            last = pe.matmul(to, left[:, b * KC + k, :], w[:, k, :],
                                             start=(k == 0), stop=(k == KC - 1 and bias is None))
                        if bias is not None:
                            last = pe.matmul(to, ones[0:1, :], bias, start=False, stop=True)
                    last.then_inc(up, 1)

                def first(n):
                    pe.wait_ge(z_t_here, n)
                    turn_rows(y, normed[0], n, y_turned)
                    pe.wait_ge(up2_here, n)
                    product(y_t, w_rff, n, y_t_here, bias_row[:, 0, :], product1)

                def second(n):
                    pe.wait_ge(y_t_here, n + 3)
                    turn_rows(z, normed[1], n, z_turned)
                    pe.wait_ge(up1_here, n + 3)
                    product(z_t, w_upd, n, z_t_here, None, product2)

                pe.wait_ge(sums_added, n_step + 2)
                first(0)

                pe.wait_ge(up1_here, 2)
                pe.wait_ge(y_t_here, 2)
                first(1)
                second(0)
                with pe.Fori(2, n_batch) as k:
                    first(k)
                    second(k - 1)
                turn_rows(z, normed[1], n_batch - 1, z_turned)
                pe.wait_ge(up2_here, n_batch)
                product(z_t, w_upd, n_batch - 1, z_t_here, None, product2)

            @block.vector
            def _(vec):
                done = [0]

                def link(ins):
                    done[0] += 1
                    ins.then_inc(v_link, 1)
                    vec.wait_ge(v_link, done[0])

                vec.nop().then_inc(sums_added, 2)
                vec.nop().then_inc(v_off, 2)
                vec.nop().then_inc(va_taken, 1)
                vec.nop().then_inc(meta_used, 1)
                vec.nop().then_inc(x_low, 1)
                vec.nop().then_inc(z_read, 1)
                vec.wait_ge(consts, 5)
                vec.tensor_scalar(ident[:, :], diff[:, :], 0.0, None, ALU.is_equal)
                vec.tensor_scalar(before[:, :], diff[:, :], 0.0, None, ALU.is_gt)
                vec.tensor_scalar(far_ident[:, :], diff[:, :], 0.0, -FAR, ALU.is_equal, ALU.mult)
                vec.tensor_scalar(upto[:, :], diff[:, :], 0.0, None, ALU.is_ge).then_inc(consts_made, 1)
                vec.wait_ge(src_in, 48)
                vec.tensor_copy(src_f[0:half, :, :], src_i[0:half, :, :]).then_inc(src_cast, 1)
                vec.memset(place, float(2 * n_row))
                vec.wait_ge(wk_in, 128)
                vec.tensor_tensor(fold[:, 0:KC, :], raw_k[:, :, :],
                                  att[:, :].unsqueeze(1).to_broadcast([P, KC, D]), ALU.mult)
                link(vec.tensor_tensor(fold[:, KC, :], b_k, att[:, :], ALU.mult))
                for k in range(KC):
                    vec.tensor_reduce(raw_va[:, k, D:VA], fold[:, k, :].rearrange("p (h c) -> p h c", h=H),
                                      AX.X, ALU.add)
                vec.tensor_reduce(b_va[:, D:VA], fold[:, KC, :].rearrange("p (h c) -> p h c", h=H),
                                  AX.X, ALU.add).then_inc(folded, 1)
                vec.wait_ge(src_turned, 1)
                for s in range(2):
                    last = vec.tensor_copy(seg_f[:, s * half:(s + 1) * half, :],
                                           ps[:, s, 0:T * half].rearrange("p (t b) -> p b t", t=T))
                link(last)
                link(vec.memset(seg_f[0:repeated // T, n_block - 1, :], float(P * (n_bin + 1))))
                link(vec.tensor_copy(seg_i, seg_f[:, :, :].rearrange("p b t -> p (b t)")))
                link(vec.tensor_scalar(bin_i, seg_i, P.bit_length() - 1, None,
                                       ALU.logical_shift_right))
                link(vec.tensor_copy(bin_h[:, :], bin_i))
                for b in range(n_bin):
                    vec.tensor_scalar(mask[:, b, :], bin_h[:, :], float(b), None, ALU.is_equal)\
                       .then_inc(masks_made, 1)
                vec.wait_ge(totals_up, 1)
                vec.tensor_copy(tot_c[0:n_bin, :], ps[0:n_bin, 2, 128:129]).then_inc(tot_c_down, 1)
                link(vec.tensor_copy(total[:, :], ps[:, 2, 64:64 + n_bin]))
                link(vec.tensor_tensor_scan(upto_bin[:, :], total[:, :], total[:, :], 0.0, ALU.add, ALU.bypass))
                link(vec.tensor_tensor(start_at[:, :], upto_bin[:, :], total[:, :], ALU.subtract))
                link(vec.tensor_tensor(start_at[:, :], start_at[:, :], ps[:, 2, 0:n_bin], ALU.add))
                nb = n_bin
                vec.wait_ge(ends_up, 1)
                vec.tensor_scalar(ends_i[0:nb, 0:1], ps[0:nb, 3, 16:17], float(BLOCK - 1), None, ALU.add)
                vec.tensor_copy(ends_i[0:nb, 1:2], ps[0:nb, 3, 17:18])
                link(vec.tensor_copy(ends_i[0:nb, 2:3], ps[0:nb, 3, 16:17]))
                lb = BLOCK.bit_length() - 1
                vec.tensor_scalar(ends_i[0:nb, 4:6], ends_i[0:nb, 0:2], lb, None, ALU.logical_shift_right)
                link(vec.tensor_scalar(ends_i[0:nb, 6:7], ends_i[0:nb, 2:3], BLOCK - 1, None, ALU.bitwise_and))
                link(vec.tensor_copy(ends[0:nb, 0:3], ends_i[0:nb, 4:7]))
                vec.tensor_tensor(steps_c[0:nb, :], ends[0:nb, 0:1], ends[0:nb, 1:2], ALU.subtract)\
                   .then_inc(steps_down, 1)
                link(vec.tensor_scalar(mid[0:nb, :], ends[0:nb, 2:3], 1.0, None, ALU.min))
                vec.tensor_scalar(mid_w[0:nb, :], ones[0:nb, :], mid[0:nb, 0:1], None, ALU.mult)
                vec.wait_ge(steps_up, 1)
                link(vec.tensor_copy(steps_in[0:nb, :], ps[0:nb, 3, 32:33]))
                vec.tensor_scalar(passed[0:nb, :], step_no[0:nb, :], steps_in[0:nb, 0:1], None, ALU.is_ge)\
                   .then_inc(passed_down, 1)
                vec.wait_ge(passed_up, 1)
                vec.tensor_copy(bin_of[:, :], ps[:, 0, 0:n_step])
                link(vec.tensor_tensor(group_of[:, :], step_no[:, :], ps[:, 1, 0:n_step], ALU.subtract))
                vec.tensor_scalar(first_seg[:, :], bin_of[:, :], float(P), None, ALU.mult)
                vec.tensor_copy(bin_of_i[:, :], bin_of[:, :])
                vec.tensor_scalar(group_of_i[:, :], group_of[:, :], float(n_block - 1), 0.0, ALU.min, ALU.max)\
                   .then_inc(steps_made, 1)
                runs = [ps[:, 4:6, :].rearrange("p a n -> p (a n)")[:, 0:n_tile],
                        ps[:, 6:8, :].rearrange("p a n -> p (a n)")[:, 0:n_tile]]

                def put(b):
                    vec.wait_ge(runs_made, b + 1)
                    vec.wait_ge(puts_made, b)
                    vec.copy_predicated(place, mask[:, b, :], runs[b % 2]).then_inc(puts_made, 1)

                for b in range(n_bin):
                    if b >= 2:
                        vec.wait_ge(puts_made, b - 1)
                    vec.tensor_tensor_scan(runs[b % 2], mask[:, b, :], mask[:, b, :], start_at[:, b:b + 1],
                                           ALU.add, ALU.bypass).then_inc(runs_made, 1)
                    if b:
                        put(b - 1)
                put(n_bin - 1)
                vec.wait_ge(puts_made, n_bin)
                vec.tensor_scalar(place_i[:, :], place, -1.0, None, ALU.add).then_inc(tables, 1)
                vec.wait_ge(folded, 1)
                vec.wait_ge(params_in, 16 * (len(params) + len(rows_of)))
                for parts, raw in ((w_in, raw_in), (w_va, raw_va)):
                    link(vec.tensor_copy(parts[0][:, :, :], raw[:, :, :]))
                    last = vec.tensor_tensor(parts[1][:, :, :], raw[:, :, :], parts[0][:, :, :].bitcast(FP32),
                                             ALU.subtract)
                last.then_inc(split, 1)
                vec.memset(hi[:, :, :], -3.0e38)
                vec.memset(lo[:, :, :], 3.0e38).then_inc(v_score, 1)

                def take_values(t, u):
                    vec.wait_ge(va_up, 2 * t + (u + 3))
                    if not isinstance(t, int) or t:
                        vec.wait_ge(sent[u], 16 * T * t)
                    vec.tensor_tensor(row[:, u, :, 0:VA], ps[:, 4:8, 0:VA],
                                      b_va[:, :].unsqueeze(1).to_broadcast([P, T, VA]), ALU.add)\
                       .then_inc(va_taken, 1)
                    vec.wait_ge(va_taken, 2 * t + (u + 2))
                    s = row[:, u, :, D:VA]
                    vec.scalar_tensor_tensor(s, s, SLOPE, s, ALU.mult, ALU.max).then_inc(row_ready, 1)
                    vec.wait_ge(row_ready, 2 * t + (u + 1))
                    vec.wait_ge(v_score, 2 * t + (u + 1))
                    vec.tensor_tensor(hi[:, :, :], hi[:, :, :], s, ALU.max)
                    vec.tensor_tensor(lo[:, :, :], lo[:, :, :], s, ALU.min).then_inc(v_score, 1)

                def edges_low(n, u):
                    vec.wait_ge(e_high, n + 1)
                    for k in range(KC):
                        last = vec.tensor_tensor(e_t[1][:, u, k, :], ps[:, k, :],
                                                 e_t[0][:, u, k, :].bitcast(FP32), ALU.subtract)
                    last.then_inc(e_low, 1)

                def hidden_low(n, u):
                    vec.wait_ge(x_whole, n + 1)
                    vec.tensor_tensor(x_t[1][:, u, :, :], x_f[:, :, :], x_t[0][:, u, :, :].bitcast(FP32),
                                      ALU.subtract).then_inc(x_low, 1)

                edges_low(0, 0)
                edges_low(1, 1)
                hidden_low(0, 0)
                for u in range(2):
                    edges_low(u + 2, u)
                    hidden_low(u + 1, 1 - u)
                    take_values(0, u)
                with vec.Fori(1, n_block // 2 - 1) as t:
                    for u in range(2):
                        edges_low(2 * t + (u + 2), u)
                        hidden_low(2 * t + (u + 1), 1 - u)
                        take_values(t, u)
                hidden_low(n_block - 1, 1)
                for u in range(2):
                    take_values(n_block // 2 - 1, u)

                vec.wait_ge(v_score, n_block + 1)
                vec.tensor_reduce(ext[:, 0:H], hi[:, :, :].rearrange("p t h -> p h t"), AX.X, ALU.max)
                link(vec.tensor_reduce(ext[:, H:2 * H], lo[:, :, :].rearrange("p t h -> p h t"), AX.X, ALU.min))
                vec.tensor_scalar(ext[:, H:2 * H], ext[:, H:2 * H], -1.0, None, ALU.mult).then_inc(ext_ready, 1)
                vec.wait_ge(ext_reduced, 1)
                vec.tensor_copy(shift[:, :, :], ext_all[:, 0:H].unsqueeze(1).to_broadcast([P, n_bin + 1, H]))
                link(vec.tensor_tensor(span[:, :], ext_all[:, 0:H], ext_all[:, H:2 * H], ALU.add))
                link(vec.tensor_reduce(span1[:, :], span[:, :], AX.X, ALU.max))
                vec.tensor_scalar(wide[:, :], span1[:, :], SPAN, None, ALU.is_gt).then_inc(wide_known, 1)
                vec.wait_ge(wide_known, 1)
                far = vec.value_load(wide[0:1, 0:1], min_val=0, max_val=1)

                def hot_half(n, here, u):
                    v = u % 2
                    vec.wait_ge(sums_up, n + 1)
                    vec.wait_ge(loaded_in[u], here)
                    for j in range(T // 2):
                        last = vec.tensor_scalar(hot[:, v, j, :], col[:, :], first_seg[:, ds(n, 1)],
                                                 loaded[:, u, j, VA:ROW], ALU.add, ALU.is_equal)
                    last.then_inc(hot_a, 1)

                def offsets(n, here, u):
                    vec.wait_ge(loaded_in[u], here)
                    if not isinstance(n, int) or n >= 2:
                        vec.wait_ge(exp_made, n - 1)
                    vec.tensor_tensor(off[:, u % 2, :, :], loaded[:, u, :, D:VA],
                                      ext_all[:, 0:H].unsqueeze(1).to_broadcast([P, T, H]), ALU.subtract)\
                       .then_inc(off_made, 1)

                def far_offsets(n, here, u):
                    v = u % 2
                    vec.wait_ge(loaded_in[u], here)
                    vec.wait_ge(shift_up, n + 3)
                    vec.tensor_tensor(off[:, v, :, :], loaded[:, u, :, D:VA],
                                      ps[:, 2 + v, 0:T * H].rearrange("p (t h) -> p t h", t=T), ALU.subtract)\
                       .then_inc(v_off, 1)
                    vec.wait_ge(v_off, n + 3)
                    vec.tensor_scalar(off[:, v, :, :], off[:, v, :, :], 0.0, None, ALU.min).then_inc(off_made, 1)

                def weigh(n, u):
                    v = u % 2
                    vec.wait_ge(exp_made, n + 1)
                    vec.tensor_tensor(
                        wv[:, v, :, 0:D].rearrange("p t (h c) -> p t h c", h=H),
                        loaded[:, u, :, 0:D].rearrange("p t (h c) -> p t h c", h=H),
                        wv[:, v, :, D:VA].unsqueeze(3).to_broadcast([P, T, H, C]), ALU.mult)\
                       .then_inc(wv_made, 1)

                def add_sums(n, v):
                    b = vec.value_load(bin_of_i[0:1, ds(n, 1)], min_val=0, max_val=n_bin)
                    vec.wait_ge(sums_up, n + 3)
                    vec.wait_ge(sums_added, n + 2)
                    vec.tensor_tensor(acc[:, b, :], acc[:, b, :], ps[:, 4 + v, 0:VA], ALU.add)\
                       .then_inc(sums_added, 1)

                vec.wait_ge(acc_clear, 1)
                with vec.If(far > 0):
                    vec.memset(shift[:, :, :], FAR).then_inc(v_max, 1)
                    with vec.Fori(0, n_step) as i:
                        b = vec.value_load(bin_of_i[0:1, ds(i, 1)], min_val=0, max_val=n_bin)
                        vec.wait_ge(meta_in, 16 * i + 16)
                        vec.tensor_tensor(seg_m[:, :], meta[:, :, H],
                                          first_seg[:, ds(i, 1)].to_broadcast([P, T]), ALU.subtract)\
                           .then_inc(v_max, 1)
                        vec.wait_ge(v_max, (2 + T) * i + 2)
                        for j in range(T):
                            last = vec.tensor_scalar(outside[:, j, :], col[:, :], seg_m[:, j:j + 1], -1.0,
                                                     ALU.not_equal, ALU.mult)
                        last.then_inc(outside_made, 1)
                        for j in range(T):
                            vec.tensor_tensor(spread, ident[:, :].unsqueeze(1).to_broadcast([P, H, P]),
                                              meta[:, j, 0:H].unsqueeze(2).to_broadcast([P, H, P]),
                                              ALU.mult).then_inc(spread_made, 1)
                            vec.wait_ge(scores_up, T * i + (j + 1))
                            vec.tensor_reduce(seg_max[:, :],
                                              ps[:, 0:2, :].rearrange("p g (h e) -> p (g h) e", e=P),
                                              AX.X, ALU.max).then_inc(v_max, 1)
                            vec.wait_ge(v_max, (2 + T) * i + (3 + j))
                            last = vec.tensor_tensor(shift[:, b, :], shift[:, b, :], seg_max[:, :], ALU.max)
                        last.then_inc(v_max, 1)
                        vec.nop().then_inc(meta_used, 1)
                    vec.memset(mid[:, :], 1.0).then_inc(shifts_known, 1)

                    def far_step(n, here, u):
                        hot_half(n, here, u)
                        far_offsets(n, here, u)
                        weigh(n, u)
                        add_sums(n, u % 2)

                    far_step(0, 16, 0)
                    with vec.Fori(0, (n_step - 1) // 4) as q:
                        for u in range(4):
                            far_step(4 * q + (u + 1), 16 * q + (32 if u == 3 else 16), (u + 1) % 4)
                with vec.Else():
                    def near_step(n, here, here_next, u):
                        if here_next is not None:
                            offsets(n + 1, here_next, (u + 1) % 4)
                        hot_half(n, here, u)
                        weigh(n, u)
                        if not isinstance(n, int) or n:
                            add_sums(n - 1, (u - 1) % 2)

                    offsets(0, 16, 0) 
                    near_step(0, 16, 16, 0)
                    with vec.Fori(0, (n_step - 5) // 4) as q:
                        for u in range(4):
                            near_step(4 * q + (u + 1), 16 * q + (32 if u == 3 else 16),
                                      16 * q + (32 if u >= 2 else 16), (u + 1) % 4)
                    for n in range(n_step - 4, n_step):
                        near_step(n, 16 * (n // 4) + 16, 16 * ((n + 1) // 4) + 16 if n + 1 < n_step else None,
                                  n % 4)
                    add_sums(n_step - 1, (n_step - 1) % 2)

                vec.wait_ge(sums_added, n_step + 2)
                done5 = [0, 0]

                def link5(ins, k=0):
                    done5[0] += 1
                    ins.then_inc(v_link5, 1)
                    vec.wait_ge(v_link5, done5[0] + k)

                def norm(to, of, n, done_, k=0):
                    for b in range(batch):
                        last = vec.bn_stats(stats[:, b, :], of[:, b, :])
                    link5(last, k)
                    vec.memset(pause[:, 1:2], 0.0)
                    for b in range(batch):
                        last = vec.bn_aggr(mv[:, b, :], stats[:, b, :])
                    last.then_inc(var_ready, 1)
                    vec.wait_ge(root_made, n + 1)
                    link5(vec.reciprocal(rstd[:, :], sd[:, :]), k)
                    for b in range(batch):
                        last = vec.tensor_scalar(to[:, b, :], of[:, b, :], mv[:, b, 0:1], rstd[:, b:b + 1],
                                                 ALU.subtract, ALU.mult)
                    last.then_inc(done_, 1)

                def part_a(k, n, off_=0):
                    s = acc[:, ds(k * batch, batch), :]
                    link5(vec.tensor_scalar(den[:, :, :], s[:, :, D:VA], DENOM_MIN, None, ALU.max), off_)
                    link5(vec.reciprocal(rec[:, :, :], den[:, :, :]), off_)
                    if not isinstance(k, int) or k:
                        vec.wait_ge(y_res_made, k)
                        vec.wait_ge(y_turned, k)
                    link5(vec.tensor_tensor(y.rearrange("p b (h c) -> p b h c", h=H),
                                            s[:, :, 0:D].rearrange("p b (h c) -> p b h c", h=H),
                                            rec[:, :, :].unsqueeze(3).to_broadcast([P, batch, H, C]), ALU.mult),
                          off_)
                    link5(vec.tensor_tensor(y, y, att[:, :].unsqueeze(1).to_broadcast([P, batch, D]), ALU.add),
                          off_)
                    norm(y, y, n, normed[0], off_)

                def part_b(k, n, off_=0):
                    vec.wait_ge(up1_here, k + 2)
                    vec.wait_ge(y_res_made, k + 1)
                    if not isinstance(k, int) or k:
                        vec.wait_ge(z_turned, k)
                    vec.scalar_tensor_tensor(z, up1, 0.0, y_res, ALU.max, ALU.add).then_inc(z_read, 1)
                    vec.wait_ge(z_read, k + 2)
                    norm(z, z, n, normed[1], off_)

                def part_c(k, n, off_=0):
                    vec.wait_ge(updated, k + 1)
                    vec.wait_ge(xr_here, 16 * k + 16 if not isinstance(k, int) or k < n_batch - 1
                                else 16 * n_batch + 16)
                    if not isinstance(k, int) or k:
                        vec.wait_ge(res_sent, 16 * k)
                    vec.scalar_tensor_tensor(res, up2, 0.0, xr, ALU.max, ALU.add).then_inc(res_made, 1)
                    vec.wait_ge(res_made, k + 1)
                    norm(res, res, n, normed[2], off_)

                part_a(0, 0)
                part_a(1, 1)
                part_b(0, 2)
                LINKS = 10
                with vec.Fori(2, n_batch) as k:
                    begin = done5[0]
                    step_ = LINKS * (k - 2)
                    part_a(k, 3 * k - 3, step_)
                    part_b(k - 1, 3 * k - 2, step_)
                    part_c(k - 2, 3 * k - 1, step_)
                    assert done5[0] - begin == LINKS
                done5[0] += LINKS * (n_batch - 3)
                part_b(n_batch - 1, 3 * n_batch - 3)
                part_c(n_batch - 2, 3 * n_batch - 2)
                part_c(n_batch - 1, 3 * n_batch - 1)


_INS = ["x", "src", "edge_attr_256", "L0_gnn_W_v2e", "L0_gnn_b_v2e", "L0_gnn_W_K", "L0_gnn_b_K",
        "L0_gnn_W_V", "L0_gnn_b_V", "L0_gnn_att_r", "L0_gnn_ln0_g", "L0_gnn_ln0_b", "L0_gnn_ln1_g",
        "L0_gnn_ln1_b", "L0_gnn_W_rff", "L0_gnn_b_rff", "L0_gnn_W_upd", "L0_gnn_b_upd"]


def kernel(**inputs):
    import numpy as np
    import concourse.bacc as bacc
    from concourse.bass_utils import run_bass_kernel_spmd

    nc = bacc.Bacc("TRN2", target_bir_lowering=False, num_devices=1)
    arrays, args = {}, []
    for name in _INS:
        a = np.ascontiguousarray(inputs[name])
        arrays[f"in_{name}"] = a
        args.append(nc.dram_tensor(f"in_{name}", a.shape, mybir.dt.from_np(a.dtype), kind="ExternalInput").ap())
    args.append(nc.dram_tensor("out_0", inputs["x"].shape, FP32, kind="ExternalOutput").ap())
    gnn_kernel(nc, *args)
    r = run_bass_kernel_spmd(nc, [arrays], core_ids=[0])
    return r.results[0]["out_0"]
```

```python
import concourse.bass as bass
from concourse import mybir
from concourse.bass import ds
from contextlib import ExitStack

FP32 = mybir.dt.float32
FP32R = mybir.dt.float32r
BF16 = mybir.dt.bfloat16
I16 = mybir.dt.int16
I32 = mybir.dt.int32
ALU = mybir.AluOpType
ACT = mybir.ActivationFunctionType
AX = mybir.AxisListType

P = 128
D = 256
KC = D // P
H = 8
C = D // H
EPS = 1e-5
SLOPE = 0.2
DENOM_MIN = 1e-16
SPAN = 30.0
FILL = -1e37
FAR = -float(2 ** 100)

T = 4
BLOCK = T * P
VA = D + H
ROW = VA + 1
LATE = 12544
BANK = 512


def gnn_kernel(nc, x, src, edge, W_v2e, b_v2e, W_K, b_K, W_V, b_V, att_r, ln0_g, ln0_b, ln1_g,
               ln1_b, W_rff, b_rff, W_upd, b_upd, out):
    n_seg = x.shape[0]
    n_edge = edge.shape[0]
    n_block = -(-n_edge // BLOCK)
    last_start = n_edge - BLOCK
    repeated = (n_block - 1) * BLOCK - last_start
    n_tile = n_block * T
    n_bin = -(-n_seg // P)
    half = n_block // 2
    n_step = -(-(n_block + n_bin - 2) // 4) * 4 + 1
    n_row = n_block * BLOCK
    assert n_bin % 4 == 1 and n_block % 4 == 0 and half <= P and repeated % T == 0
    batch = 7
    n_batch = n_bin // batch
    halves = [(0, 4), (4, batch)]
    assert n_batch * batch == n_bin
    act_bins = [b for b in range(n_bin) if b % 7 < 4]
    vec_bins = [b for b in range(n_bin) if b % 7 >= 4]
    early_x = 16
    assert early_x % 4 == 0 and 2 * early_x >= len(act_bins)
    short = n_seg - (n_bin - 1) * P

    rows = nc.dram_tensor("binned_rows", (n_row, ROW), FP32).ap()
    rows_g = rows.rearrange("(g p t) d -> g p (t d)", p=P, t=T)
    rows_m = rows.rearrange("(g p t) d -> g p t d", p=P, t=T)
    x_upd = nc.dram_tensor("x_update", (n_bin * P, D), FP32).ap()
    edge_b = edge[0:(n_block - 1) * BLOCK, :].rearrange("(b p t) d -> b p (t d)", p=P, t=T)
    edge_last = edge[last_start:n_edge, :].rearrange("(p t) d -> p (t d)", t=T)

    ctx = ExitStack()
    with ctx:
        def sb(name, shape, dt=FP32):
            return ctx.enter_context(nc.sbuf_tensor(name, shape, dt))

        def sem(name):
            return ctx.enter_context(nc.semaphore(name))

        w_in = [sb(f"w_in{n}", [P, KC, D], FP32R) for n in range(2)]
        w_va = [sb(f"w_va{n}", [P, KC, VA], FP32R) for n in range(2)]
        w_rff = sb("w_rff", [P, KC, D])
        w_upd = sb("w_upd", [P, 2 * KC, D])
        cols_in = sb("cols_in", [5 * KC, P])
        cols = sb("cols", [P, 5, KC])
        att = sb("att", [P, D])
        b_va = sb("b_va", [P, VA])
        g0, c0, b_u = sb("g0", [P, D]), sb("c0", [P, D]), sb("b_u", [P, D])
        bias_row = sb("bias_row", [1, D])
        bias_parts = [sb(f"bias_part{n}", [1, D], FP32R) for n in range(2)]
        one_row = sb("one_row", [1, P], FP32R)
        col = sb("col", [P, P])
        diff = sb("diff", [P, P])
        ident = sb("ident", [P, P])
        before = sb("before", [P, P])
        upto = sb("upto", [P, P])
        ones = sb("ones", [P, P])
        eps, nought = sb("eps", [P, 1]), sb("nought", [P, 1])
        step_no = sb("step_no", [P, n_step])
        far_ident = sb("far_ident", [P, P], BF16)
        seg_f = sb("seg_f", [P, n_block, T])
        bin_h = sb("bin_h", [P, n_tile], BF16)
        place_i = sb("place_i", [P, n_tile], I32)
        spare = sb("spare", [P, 2, n_tile], BF16)
        count = sb("count", [P, n_bin])
        total = sb("total", [P, n_bin])
        upto_bin = sb("upto_bin", [P, n_bin])
        start_at = sb("start_at", [P, n_bin])
        tot_c = sb("tot_c", [P, 1])
        ends = sb("ends", [P, 4])
        ends_i = sb("ends_i", [P, 8], I32)
        mid = sb("mid", [P, 1])
        mid_w = sb("mid_w", [P, P])
        steps_c = sb("steps_c", [P, 1])
        steps_in = sb("steps_in", [P, 1])
        passed = sb("passed", [P, n_step])
        bin_of = sb("bin_of", [P, n_step])
        first_seg = sb("first_seg", [P, n_step])
        group_of = sb("group_of", [P, n_step])
        bin_of_i = sb("bin_of_i", [P, n_step], I32)
        group_of_i = sb("group_of_i", [P, n_step], I32)

        sums_w = (n_bin + 1) * VA
        early = sb("early", [P, n_bin * n_tile // 2])
        mask = early[:, :].bitcast(I16).rearrange("p (b t) -> p b t", b=n_bin)
        acc = early[:, 0:sums_w].rearrange("p (b v) -> p b v", v=VA)
        late = sb("late", [P, LATE])
        lows = sb("lows", [P, 16 * BLOCK], FP32R)

        def cutter(region, start, end):
            at_ = [start]

            def take(*shape):
                n = 1
                for k in shape:
                    n *= k
                at_[0] += n
                assert at_[0] <= end
                v = region[:, at_[0] - n:at_[0]]
                names = "abc"[:len(shape)]
                if len(shape) == 1:
                    return v
                return v.rearrange(f"p ({' '.join(names)}) -> p {' '.join(names)}",
                                   **{m: k for m, k in zip(names, shape)})
            return take

        take = cutter(late, 0, LATE)
        src_i = take(2, BLOCK).bitcast(I32)
        src_f = take(2, BLOCK)
        seg_i = take(n_tile).bitcast(I32)
        bin_i = take(n_tile).bitcast(I32)
        place = take(n_tile)
        fold = take(KC + 1, D)
        b_k = take(D)
        x_in = take(4, D)
        x_turned = take(2, KC, P)
        x_made = take(4, D)
        raw_in, raw_k, raw_va = take(KC, D), take(KC, D), take(KC, VA)
        x_f = take(KC, BLOCK)
        fill = take(T * ROW)
        runs = late[:, 0:4 * n_tile].rearrange("p (s t) -> p s t", s=4)
        assert 4 * n_tile <= 4 * BLOCK + 2 * n_tile
        take = cutter(early, sums_w, n_bin * n_tile // 2)
        e_in = take(4, T * D)
        row = late[:, 0:2 * T * ROW].rearrange("p (s t d) -> p s t d", s=2, t=T)
        take = cutter(lows, 0, 16 * BLOCK)
        e_t = [take(2, KC, BLOCK) for n in range(2)]
        x_t = [take(2, KC, BLOCK) for n in range(2)]
        take = cutter(early, sums_w, n_bin * n_tile // 2)
        loaded = take(4, T, ROW)
        take = cutter(late, 0, LATE)
        hot = take(4, T, P)
        hot_t = take(2, T, P)
        wv = take(4, T, VA)
        spread = take(H, P)
        take = cutter(early, sums_w, n_bin * n_tile // 2)
        xr, xu, res = take(batch, D), take(batch, D), take(batch, D)
        take = cutter(late, 0, LATE)
        y, y_res, z = take(batch, D), take(batch, D), take(batch, D)
        up1, up2 = take(batch, D), take(batch, D)
        y_t, z_t = take(batch * KC, P), take(batch * KC, P)
        den = sb("den", [P, batch, H])
        rec = sb("rec", [P, batch, H])
        stats = sb("stats", [P, 3, batch, 6])
        mv = sb("mv", [P, 3, batch, 2])
        sd = sb("sd", [P, 3, batch])
        rstd = sb("rstd", [P, 3, batch])
        less = sb("less", [P, batch])
        at = sb("at", [P, 2, T], I32)
        hi, lo = sb("hi", [P, T, H]), sb("lo", [P, T, H])
        ext = sb("ext", [P, 2 * H])
        ext_all = sb("ext_all", [P, 2 * H])
        top = sb("top", [P, 2])
        minus_top = sb("minus_top", [P, 1])
        wide = sb("wide", [P, 1], I32)
        shift = sb("shift", [P, n_bin + 1, H])
        meta = sb("meta", [P, T, H + 1])
        seg_m = sb("seg_m", [P, T])
        outside = sb("outside", [P, T, P], BF16)
        seg_max = sb("seg_max", [P, H])
        pause = sb("pause", [P, 2])
        from_seg = sb("from_seg", [P, 4])
        behind = sb("behind", [P, 2])
        apart = sb("apart", [P, 2, P])
        off = sb("off", [P, 2, T, H])

        ps = ctx.enter_context(nc.psum_tensor("ps", [P, 8, BANK], FP32))

        def sems(name, n):
            return [sem(f"{name}{k}") for k in range(n)]

        consts, consts_made = sem("consts"), sem("consts_made")
        params_in, wk_in = sem("params_in"), sem("wk_in")
        cols_turned, cols_here = sem("cols_turned"), sem("cols_here")
        folded, split = sem("folded"), sem("split")
        src_in, src_cast, src_turned = sem("src_in"), sem("src_cast"), sem("src_turned")
        v_link = sem("v_link")
        masks_made = sem("masks_made")
        counted, counted_too = sem("counted"), sem("counted_too")
        totals_up, tot_c_down, starts_made = sem("totals_up"), sem("tot_c_down"), sem("starts_made")
        ends_up = sem("ends_up")
        steps_down, steps_up, steps_made = sem("steps_down"), sem("steps_up"), sem("steps_made")
        passed_down, passed_up = sem("passed_down"), sem("passed_up")
        runs_made, puts_made, tables = sem("runs_made"), sem("puts_made"), sem("tables")
        fill_set, filled = sem("fill_set"), sem("filled")
        xt_here, xt_turned, xt_down = sems("xt_here", 4), sem("xt_turned"), sem("xt_down")
        xt_up, xt_out, xt_stored = sem("xt_up"), sem("xt_out"), sems("xt_stored", 4)
        e_here, e_turned, e_high, e_low = sems("e_here", 4), sem("e_turned"), sem("e_high"), sem("e_low")
        x_up, x_high, x_whole, x_low = sem("x_up"), sem("x_high"), sem("x_whole"), sem("x_low")
        va_up, va_taken, row_ready = sem("va_up"), sem("va_taken"), sem("row_ready")
        v_score, row_meta, sent = sem("v_score"), sem("row_meta"), sems("sent", 2)
        acc_clear = sem("acc_clear")
        ext_ready, ext_reduced, wide_known = sem("ext_ready"), sem("ext_reduced"), sem("wide_known")
        meta_in, meta_used = sem("meta_in"), sem("meta_used")
        v_max, outside_made, spread_made = sem("v_max"), sem("outside_made"), sem("spread_made")
        scores_up, shifts_known = sem("scores_up"), sem("shifts_known")
        loaded_in, from_made = sems("loaded_in", 4), sem("from_made")
        hot_a, hot_b, hot_c = sem("hot_a"), sem("hot_b"), sem("hot_c")
        behind_made, apart_made = sem("behind_made"), sem("apart_made")
        hot_turned, hot_t_here, shift_up = sem("hot_turned"), sem("hot_t_here"), sem("shift_up")
        v_off, off_made, exp_made, wv_made = sem("v_off"), sem("off_made"), sem("exp_made"), sem("wv_made")
        sums_up, sums_added = sem("sums_up"), sem("sums_added")
        v_link5, p_link = sem("v_link5"), sem("p_link")
        var_ready, root_made, normed = sem("var_ready"), sem("root_made"), sems("normed", 3)
        scale_made = sem("scale_made")
        y_turned, y_t_here, y_res_made = sem("y_turned"), sem("y_t_here"), sem("y_res_made")
        z_read, z_turned, z_t_here = sem("z_read"), sem("z_turned"), sem("z_t_here")
        product1, product2 = sem("product1"), sem("product2")
        up1_here, up2_here = sem("up1_here"), sem("up2_here")
        xr_here, xu_here, xu_biased = sem("xr_here"), sem("xu_here"), sem("xu_biased")
        updated, res_made, res_sent = sem("updated"), sem("res_made"), sem("res_sent")

        params = [
            (raw_in[:, :, :], W_v2e.rearrange("(k p) n -> p k n", p=P)),
            (raw_va[:, :, 0:D], W_V.rearrange("(k p) n -> p k n", p=P)),
            (w_rff[:, :, :], W_rff.rearrange("(k p) n -> p k n", p=P)),
            (w_upd[:, :, :], W_upd.rearrange("(k p) n -> p k n", p=P)),
            (bias_row[:, :], b_rff.rearrange("(o n) -> o n", o=1)),
        ]
        rows_of = [(b_va[:, 0:D], b_V), (g0[:, :], ln0_g), (c0[:, :], ln0_b), (b_u[:, :], b_upd)]

        def every(v):
            return v.rearrange("(o n) -> o n", o=1).broadcast_to([P, v.shape[0]])

        def turn_of(n):
            return n_bin - 1 - n

        with nc.Block() as block:

            @block.sync
            def _(sp):
                sp.dma_start(src_i[0:half, 0, :],
                             src[0:half * BLOCK].rearrange("(b n) -> b n", n=BLOCK)).then_inc(src_in, 16)
                sp.dma_start(src_i[0:half - 1, 1, :],
                             src[half * BLOCK:(n_block - 1) * BLOCK].rearrange("(b n) -> b n", n=BLOCK))\
                  .then_inc(src_in, 16)
                sp.dma_start(src_i[half - 1:half, 1, :],
                             src[last_start:n_edge].rearrange("(b n) -> b n", n=BLOCK)).then_inc(src_in, 16)
                for dst, of in params:
                    sp.dma_start(dst, of).then_inc(params_in, 16)
                for dst, of in rows_of:
                    sp.dma_start(dst, every(of)).then_inc(params_in, 16)
                x_b = x[0:(n_bin - 1) * P, :].rearrange("(b p) d -> b p d", p=P)
                xu_b = x_upd.rearrange("(b p) d -> b p d", p=P)

                def load_x(of, part, u):
                    sp.dma_start(x_in[part, u, :], of).then_inc(xt_here[u], 16)

                def store_x(b, u, n):
                    sp.wait_ge(xt_out, n + 3)
                    sp.dma_start(xu_b[b], x_made[:, u, :]).then_inc(xt_stored[u], 16)

                everyone = slice(0, P)
                for n in range(4):
                    load_x(x_b[n], everyone, n)
                with sp.Fori(0, (n_bin - 5) // 4) as t:
                    for u in range(4):
                        sp.wait_ge(xt_turned, 4 * t + (u + 1))
                        load_x(x_b[4 * t + (u + 4)], everyone, u)
                        store_x(4 * t + u, u, 4 * t + u)
                sp.wait_ge(xt_turned, n_bin - 4)
                load_x(x[(n_bin - 1) * P:n_seg, :], slice(0, short), 0)
                store_x(n_bin - 5, 0, n_bin - 5)
                for n in range(n_bin - 4, n_bin):
                    store_x(n, n % 4, n)
                sp.wait_ge(puts_made, n_bin - sums_w // (n_tile // 2))
                def load_block(of, u):
                    sp.dma_start(e_in[:, u, :], of).then_inc(e_here[u], 16)

                for n in range(4):
                    load_block(edge_b[n], n)
                with sp.Fori(1, n_block // 4 - 1) as t:
                    for u in range(4):
                        sp.wait_ge(e_turned, 4 * t + (u - 3))
                        load_block(edge_b[4 * t + u], u)
                for n in range(n_block - 4, n_block):
                    sp.wait_ge(e_turned, n - 3)
                    load_block(edge_b[n] if n < n_block - 1 else edge_last, n % 4)
                for u in range(2):
                    sp.wait_ge(sent[u], 16 * T * (n_block // 2))
                sp.wait_ge(filled, 16)
                sp.wait_ge(wide_known, 1)
                far = sp.value_load(wide[0:1, 0:1], min_val=0, max_val=1)
                with sp.If(far > 0):
                    with sp.Fori(0, n_step) as i:
                        sp.wait_ge(meta_used, i + 1)
                        g = sp.value_load(group_of_i[0:1, ds(i, 1)], min_val=0, max_val=n_block - 1)
                        sp.dma_start(meta[:, :, :], rows_m[g][:, :, D:ROW]).then_inc(meta_in, 16)
                def load_step(n, u):
                    g = sp.value_load(group_of_i[0:1, ds(n, 1)], min_val=0, max_val=n_block - 1)
                    sp.dma_start(loaded[:, u, :, :].rearrange("p t d -> p (t d)"), rows_g[g])\
                      .then_inc(loaded_in[u], 16)
                for n in range(4):
                    load_step(n, n)
                sp.wait_ge(wv_made, 1)
                sp.wait_ge(hot_b, 1)
                sp.wait_ge(hot_c, 1)
                load_step(4, 0)
                with sp.Fori(0, (n_step - 5) // 4) as q:
                    for u in range(4):
                        sp.wait_ge(wv_made, 4 * q + (u + 2))
                        sp.wait_ge(hot_b, 4 * q + (u + 2))
                        sp.wait_ge(hot_c, 4 * q + (u + 2))
                        load_step(4 * q + (u + 5), (u + 1) % 4)
                full = (n_bin - 1) * P

                def batch_rows(t, k):
                    return t[0:(t.shape[0] // P) * P, :].rearrange("(b p) d -> p b d", p=P)\
                        [:, ds(k * batch, batch), :]

                def store_batch(k, n):
                    sp.wait_ge(normed[2], n + 1)
                    sp.dma_start(batch_rows(out, k), res).then_inc(res_sent, 16)

                sp.wait_ge(sums_added, n_step + 4)
                for u in range(4):
                    sp.wait_ge(xt_stored[u], 16 * ((n_bin + 3 - u) // 4))
                sp.dma_start(xr, batch_rows(x, 0)).then_inc(xr_here, 16)
                sp.dma_start(xu, batch_rows(x_upd, 0)).then_inc(xu_here, 16)
                with sp.Fori(0, n_batch - 2) as k:
                    sp.wait_ge(res_made, k + 2)
                    sp.dma_start(xr, batch_rows(x, k + 1)).then_inc(xr_here, 16)
                    sp.dma_start(xu, batch_rows(x_upd, k + 1)).then_inc(xu_here, 16)
                    store_batch(k, k)
                sp.wait_ge(res_made, n_batch)
                k = n_batch - 1
                sp.dma_start(xu, batch_rows(x_upd, k)).then_inc(xu_here, 16)
                sp.dma_start(xr[:, 0:batch - 1, :],
                             x[k * batch * P:full, :].rearrange("(b p) d -> p b d", p=P)).then_inc(xr_here, 16)
                sp.dma_start(xr[0:short, batch - 1, :], x[full:n_seg, :]).then_inc(xr_here, 16)
                store_batch(n_batch - 2, n_batch - 2)
                sp.wait_ge(normed[2], n_batch)
                sp.dma_start(out[k * batch * P:full, :].rearrange("(b p) d -> p b d", p=P),
                             res[:, 0:batch - 1, :]).then_inc(res_sent, 16)
                sp.dma_start(out[full:n_seg, :], res[0:short, batch - 1, :]).then_inc(res_sent, 16)
                sp.wait_ge(res_sent, 16 * (n_batch + 1))

            @block.gpsimd
            def _(pool):
                pool.iota(col[:, :], [[1, P]], base=0, channel_multiplier=0,
                          allow_small_or_imprecise_dtypes=True).then_inc(consts, 1)
                pool.iota(diff[:, :], [[1, P]], base=0, channel_multiplier=-1,
                          allow_small_or_imprecise_dtypes=True).then_inc(consts, 1)
                pool.iota(step_no[:, :], [[1, n_step]], base=0, channel_multiplier=0,
                          allow_small_or_imprecise_dtypes=True).then_inc(consts, 1)
                pool.memset(ones[:, :], 1.0).then_inc(consts, 1)
                pool.memset(eps[:, :], EPS).then_inc(consts, 1)
                pool.memset(nought[:, :], 0.0).then_inc(consts, 1)
                pool.memset(fill, FILL).then_inc(fill_set, 1)
                pool.wait_ge(fill_set, 1)
                pool.dma_start(rows[n_edge:n_row, :].rearrange("(p t) d -> p (t d)", t=T),
                               fill[0:(n_row - n_edge) // T, :]).then_inc(filled, 16)
                pool.wait_ge(filled, 16)

                pool.wait_ge(tables, 1)
                limit, bound = pool.alloc_register("limit"), pool.alloc_register("bound")
                pool.reg_mov(limit, n_row - 2)
                pool.reg_mov(bound, n_row - 1)

                def send(t, u):
                    if not isinstance(t, int):
                        pool.wait_ge(sent[u], 16 * T * t)
                    pool.tensor_copy(at[:, u, :], place_i[:, ds((2 * t + u) * T, T)]).then_inc(row_meta, 1)
                    pool.tensor_copy(row[:, u, :, VA:ROW],
                                     seg_f[:, ds(2 * t + u, 1), :].rearrange("p o t -> p t o"))\
                        .then_inc(row_meta, 1)
                    pool.wait_ge(row_ready, 2 * t + u + 1)
                    pool.wait_ge(row_meta, 4 * t + 2 * u + 2)
                    pool.reg_add(bound, limit, 1)
                    for j in range(T):
                        pool.indirect_dma_start(
                            rows, bass.IndirectOffsetOnAxis(ap=at[:, u, j:j + 1], axis=0),
                            row[:, u, j, :], None, bounds_check=bound, oob_is_err=False)\
                            .then_inc(sent[u], 16)

                for b in (0, n_bin):
                    pool.memset(acc[:, b, :], 0.0).then_inc(acc_clear, 1)
                for u in range(2):
                    send(0, u)
                with pool.Fori(1, n_bin) as t:
                    pool.tensor_copy(acc[:, ds(t, 1), :].rearrange("p o v -> p (o v)"),
                                     nought[:, 0:1].to_broadcast([P, VA])).then_inc(acc_clear, 1)
                    for u in range(2):
                        send(t, u)
                with pool.Fori(n_bin, n_block // 2) as t:
                    for u in range(2):
                        send(t, u)
                pool.wait_ge(ext_ready, 1)
                pool.partition_all_reduce(ext_all[:, :], ext[:, :], P, bass.bass_isa.ReduceOp.max)\
                    .then_inc(ext_reduced, 1)
                def hot_second(n, here, u):
                    pool.wait_ge(sums_up, n + 1)
                    pool.tensor_copy(from_seg[:, u:u + 1], first_seg[:, ds(n, 1)]).then_inc(from_made, 1)
                    pool.wait_ge(loaded_in[u], here)
                    pool.wait_ge(from_made, n + 1)
                    pool.tensor_tensor(pause[:, 0:1], eps[:, :], eps[:, :], ALU.add)
                    pool.tensor_scalar(hot[:, u, 1, :], col[:, :], from_seg[:, u:u + 1],
                                       loaded[:, u, 1, VA:ROW], ALU.add, ALU.is_equal).then_inc(hot_b, 1)

                hot_second(0, 16, 0)
                with pool.Fori(0, (n_step - 1) // 4) as q:
                    for u in range(4):
                        hot_second(4 * q + (u + 1), 16 * q + (32 if u == 3 else 16), (u + 1) % 4)

                pool.wait_ge(sums_added, n_step + 4)

                def affine(n):
                    pool.wait_ge(normed[0], n + 1)
                    pool.wait_ge(z_read, n + 1)
                    pool.tensor_tensor(y_res, y, g0[:, :].unsqueeze(1).to_broadcast([P, batch, D]),
                                       ALU.mult).then_inc(p_link, 1)
                    pool.wait_ge(p_link, n + 1)
                    pool.tensor_tensor(y_res, y_res, c0[:, :].unsqueeze(1).to_broadcast([P, batch, D]),
                                       ALU.add).then_inc(y_res_made, 1)

                def bias_update(n):
                    pool.wait_ge(xu_here, 16 * n + 16)
                    pool.tensor_tensor(xu, xu, b_u[:, :].unsqueeze(1).to_broadcast([P, batch, D]), ALU.add)\
                        .then_inc(xu_biased, 1)

                def add_update(n):
                    pool.wait_ge(up2_here, n + 2)
                    pool.wait_ge(xu_biased, n + 1)
                    pool.tensor_tensor(up2, up2, xu, ALU.add).then_inc(updated, 1)

                affine(0)
                bias_update(0)
                affine(1)
                with pool.Fori(2, n_batch) as k:
                    add_update(k - 2)
                    affine(k)
                    bias_update(k - 1)
                add_update(n_batch - 2)
                bias_update(n_batch - 1)
                add_update(n_batch - 1)

            @block.scalar
            def _(act):
                act.nop().then_inc(hot_t_here, 1)
                act.nop().then_inc(y_t_here, 2)
                act.nop().then_inc(z_t_here, 2)
                act.nop().then_inc(up1_here, 1)
                act.nop().then_inc(up2_here, 1)
                act.nop().then_inc(xt_down, 1)
                act.nop().then_inc(xt_out, 2)
                act.dma_start(raw_k[:, :, :], W_K.rearrange("(k p) n -> p k n", p=P)).then_inc(wk_in, 16)
                act.dma_start(att[:, :], every(att_r.rearrange("a h c -> (a h c)"))).then_inc(wk_in, 16)
                act.dma_start(b_k, every(b_K)).then_inc(wk_in, 16)
                for n, v in enumerate((b_v2e, ln0_g, ln0_b, ln1_g, ln1_b)):
                    act.dma_start(cols_in[n * KC:(n + 1) * KC, :], v.rearrange("(k p) -> k p", p=P))\
                       .then_inc(wk_in, 16)
                act.wait_ge(cols_turned, 1)
                act.activation(cols[:, :, :], ps[:, 3, 0:5 * KC].rearrange("p (n k) -> p n k", k=KC),
                               ACT.Copy).then_inc(cols_here, 1)
                def take_x(n, u):
                    act.wait_ge(xt_turned, n + 1)
                    act.activation(x_turned[:, u, :, :], ps[:, u, 0:KC * P].rearrange("p (k e) -> p k e", k=KC),
                                   ACT.Copy).then_inc(xt_down, 1)

                def take_update(n, u, stored):
                    if not isinstance(stored, int) or stored:
                        act.wait_ge(xt_stored[u], stored)
                    act.wait_ge(xt_up, n + 1)
                    act.activation(x_made[:, u, :], ps[:, 2 + u % 2, 0:D], ACT.Copy).then_inc(xt_out, 1)

                def early_update(n):
                    if n < early_x:
                        take_x(n, n % 2)
                    if n:
                        take_update(n - 1, (n - 1) % 4, 16 * ((n - 1) // 4))

                for n, b in enumerate(act_bins):
                    act.wait_ge(masks_made, b + 1)
                    if n >= 2:
                        act.wait_ge(counted, n - 1)
                    act.activation(spare[:, n % 2, :], mask[:, b, :], ACT.Copy, accum_out=count[:, b:b + 1])\
                       .then_inc(counted, 1)
                    if n % 2:
                        early_update(n // 2)
                for n in range(len(act_bins) // 2, early_x + 1):
                    early_update(n)
                take_x(early_x, 0)
                with act.Fori(early_x // 4, (n_bin - 1) // 4) as t:
                    for u in range(4):
                        take_x(4 * t + (u + 1), (u + 1) % 2)
                        take_update(4 * t + u, u, 16 * t)
                take_update(n_bin - 1, 0, 16 * ((n_bin - 1) // 4))
                act.wait_ge(cols_here, 1)

                def edges_high(n, u):
                    act.wait_ge(e_turned, n + 1)
                    act.wait_ge(x_up, n + 1)
                    for k in range(KC):
                        last = act.activation(e_t[0][:, u, k, :], ps[:, k, :], ACT.Copy)
                    last.then_inc(e_high, 1)

                def hidden_high(n, u):
                    act.wait_ge(x_up, n + 3)
                    act.wait_ge(va_up, n + 1)
                    for k in range(KC):
                        last = act.activation(x_t[0][:, u, k, :], ps[:, 2 + k, :], ACT.Relu,
                                              bias=cols[:, 0, k:k + 1])
                    last.then_inc(x_high, 1)
                    act.wait_ge(x_low, n + 1)
                    for k in range(KC):
                        last = act.activation(x_f[:, k, :], ps[:, 2 + k, :], ACT.Relu,
                                              bias=cols[:, 0, k:k + 1])
                    last.then_inc(x_whole, 1)

                edges_high(0, 0)
                with act.Fori(0, n_block // 2 - 1) as t:
                    for u in range(2):
                        edges_high(2 * t + (u + 1), 1 - u)
                        hidden_high(2 * t + u, u)
                edges_high(n_block - 1, 1)
                hidden_high(n_block - 2, 0)
                hidden_high(n_block - 1, 1)

                def hot_others(n, here, u):
                    act.wait_ge(loaded_in[u], here)
                    act.wait_ge(from_made, n + 1)
                    act.activation(behind[:, :], loaded[:, u, 2:T, VA], ACT.Identity, scale=-1.0,
                                   bias=from_seg[:, u:u + 1]).then_inc(behind_made, 1)
                    act.wait_ge(behind_made, n + 1)
                    for j in range(2):
                        last = act.activation(apart[:, j, :], col[:, :], ACT.Abs, bias=behind[:, j:j + 1])
                    last.then_inc(apart_made, 1)
                    act.wait_ge(sums_up, n + 1)
                    act.wait_ge(apart_made, n + 1)
                    act.activation(hot[:, u, 2:T, :], apart[:, :, :], ACT.Relu, scale=-1.0, bias=ones[:, 0:1])\
                       .then_inc(hot_c, 1)

                def exps(n, here, u):
                    act.wait_ge(loaded_in[u], here)
                    act.wait_ge(sums_up, n + 1)
                    act.activation(wv[:, u, :, D:VA], loaded[:, u, :, D:VA], ACT.Exp, bias=minus_top[:, 0:1])\
                       .then_inc(exp_made, 1)

                def far_exps(n, u):
                    act.wait_ge(off_made, n + 1)
                    act.wait_ge(sums_up, n + 1)
                    act.activation(wv[:, u, :, D:VA], off[:, u % 2, :, :], ACT.Exp).then_inc(exp_made, 1)

                def turned_hot(n, v):
                    act.wait_ge(hot_turned, n + 1)
                    act.wait_ge(shift_up, n + 1)
                    act.activation(hot_t[:, v, :, :], ps[:, v, :].rearrange("p (t e) -> p t e", t=T),
                                   ACT.Copy).then_inc(hot_t_here, 1)

                act.wait_ge(wide_known, 1)
                far = act.value_load(wide[0:1, 0:1], min_val=0, max_val=1)
                with act.If(far > 0):
                    hot_others(0, 16, 0)
                    turned_hot(0, 0)
                    far_exps(0, 0)
                    with act.Fori(0, (n_step - 1) // 4) as q:
                        for u in range(4):
                            act.wait_ge(hot_c, 4 * q + (u + 1))
                            hot_others(4 * q + (u + 1), 16 * q + (32 if u == 3 else 16), (u + 1) % 4)
                            turned_hot(4 * q + (u + 1), (u + 1) % 2)
                            far_exps(4 * q + (u + 1), (u + 1) % 4)
                with act.Else():
                    exps(0, 16, 0)
                    hot_others(0, 16, 0)
                    with act.Fori(0, (n_step - 1) // 4) as q:
                        for u in range(4):
                            exps(4 * q + (u + 1), 16 * q + (32 if u == 3 else 16), (u + 1) % 4)
                            act.wait_ge(hot_c, 4 * q + (u + 1))
                            hot_others(4 * q + (u + 1), 16 * q + (32 if u == 3 else 16), (u + 1) % 4)

                def root(n, w):
                    act.wait_ge(var_ready, n + 1)
                    act.activation(sd[:, w, :], mv[:, w, :, 1], ACT.Sqrt, bias=eps[:, 0:1]).then_inc(root_made, 1)

                def norm_res(n):
                    act.wait_ge(scale_made, n + 1)
                    for b in range(batch):
                        last = act.activation(res[:, b, :], res[:, b, :], ACT.Identity, scale=rstd[:, 2, b:b + 1],
                                              bias=less[:, b:b + 1])
                    last.then_inc(normed[2], 1)

                def take_turned(to, turned, here, n, func, c):
                    of = ps[:, 0:4, :].rearrange("p a n -> p (a n)")[:, 0:batch * KC * P]\
                        .rearrange("p (b k n) -> p k b n", k=KC, n=P)
                    to = to.rearrange("p (b k) n -> p k b n", k=KC)
                    for h, (b0, b1) in enumerate(halves):
                        act.wait_ge(turned, 2 * n + (h + 1))
                        for k in range(KC):
                            last = act.activation(to[:, k, b0:b1, :], of[:, k, b0:b1, :], func,
                                                  bias=cols[:, c + 1, k:k + 1], scale=cols[:, c, k:k + 1])
                        last.then_inc(here, 1)

                def take_product(to, up, here, n):
                    act.wait_ge(up, n + 1)
                    act.activation(to, ps[:, 4:8, :].rearrange("p a n -> p (a n)")[:, 0:batch * D]
                                   .rearrange("p (b n) -> p b n", n=D), ACT.Copy).then_inc(here, 1)

                def first_turned(n):
                    take_turned(y_t, y_turned, y_t_here, n, ACT.Identity, 1)

                def first_product(n):
                    act.wait_ge(z_read, n + 1)
                    take_product(up1, product1, up1_here, n)

                def second_turned(n):
                    take_turned(z_t, z_turned, z_t_here, n, ACT.Relu, 3)

                def second_product(n):
                    act.wait_ge(res_made, n + 1)
                    take_product(up2, product2, up2_here, n)

                root(0, 0)
                first_turned(0)
                root(1, 0)
                first_product(0)
                root(2, 1)
                first_turned(1)
                first_product(1)
                second_turned(0)
                with act.Fori(2, n_batch) as k:
                    root(3 * k - 3, 0)
                    second_product(k - 2)
                    root(3 * k - 2, 1)
                    first_turned(k)
                    root(3 * k - 1, 2)
                    first_product(k)
                    second_turned(k - 1)
                    norm_res(k - 2)
                root(3 * n_batch - 3, 1)
                second_product(n_batch - 2)
                second_turned(n_batch - 1)
                root(3 * n_batch - 2, 2)
                norm_res(n_batch - 2)
                second_product(n_batch - 1)
                root(3 * n_batch - 1, 2)
                norm_res(n_batch - 1)

            @block.tensor
            def _(pe):
                pe.nop().then_inc(x_up, 2)
                pe.nop().then_inc(va_up, 2)
                pe.nop().then_inc(sums_up, 4)
                pe.nop().then_inc(shift_up, 2)
                pe.wait_ge(consts_made, 1)
                pe.wait_ge(src_cast, 1)
                for s in range(2):
                    for j in range(T):
                        last = pe.transpose(
                            ps[:, s, j * half:(j + 1) * half],
                            src_f[0:half, s, :].rearrange("b (p t) -> b t p", t=T)[:, j, :],
                            ident[0:half, 0:half])
                last.then_inc(src_turned, 1)
                pe.wait_ge(wk_in, 128)
                pe.transpose(ps[:, 3, 0:5 * KC], cols_in[:, :], ident[0:5 * KC, 0:5 * KC])\
                  .then_inc(cols_turned, 1)
                def turn_x(n, here, u):
                    pe.wait_ge(xt_here[u], here)
                    pe.wait_ge(xt_down, n)
                    for k in range(KC):
                        last = pe.transpose(ps[:, u % 2, k * P:(k + 1) * P], x_in[:, u, k * P:(k + 1) * P],
                                            ident[:, :])
                    last.then_inc(xt_turned, 1)

                def update_x(n, u):
                    pe.wait_ge(xt_down, n + 2)
                    pe.wait_ge(xt_out, n + 1)
                    for k in range(KC):
                        last = pe.matmul(ps[:, 2 + u % 2, 0:D], x_turned[:, u % 2, k, :], w_upd[:, KC + k, :],
                                         start=(k == 0), stop=(k == KC - 1))
                    last.then_inc(xt_up, 1)

                pe.wait_ge(masks_made, 1)
                pe.wait_ge(cols_here, 1)
                pe.wait_ge(params_in, 16 * (len(params) + len(rows_of)))
                turn_x(0, 16, 0)
                with pe.Fori(0, early_x // 4 - 1) as t:
                    for u in range(4):
                        turn_x(4 * t + (u + 1), 16 * t + (32 if u == 3 else 16), (u + 1) % 4)
                        update_x(4 * t + u, u)
                for n in range(early_x - 4, early_x):
                    if n < early_x - 1:
                        turn_x(n + 1, 16 * ((n + 1) // 4) + 16, (n + 1) % 4)
                    update_x(n, n % 4)
                pe.wait_ge(xt_out, early_x + 2)
                pe.wait_ge(counted, len(act_bins))
                pe.wait_ge(counted_too, len(vec_bins))
                pe.matmul(ps[:, 2, 0:n_bin], before[:, :], count[:, :], start=True, stop=True)
                pe.matmul(ps[:, 2, 64:64 + n_bin], ones[:, :], count[:, :], start=True, stop=True)
                pe.matmul(ps[0:n_bin, 2, 128:129], count[:, :], ones[:, 0:1], start=True, stop=True)\
                  .then_inc(totals_up, 1)
                nb = n_bin
                pe.wait_ge(tot_c_down, 1)
                pe.matmul(ps[0:nb, 3, 16:17], upto[0:nb, 0:nb], tot_c[0:nb, :], start=True, stop=True)
                pe.matmul(ps[0:nb, 3, 17:18], before[0:nb, 0:nb], tot_c[0:nb, :], start=True, stop=True)\
                  .then_inc(ends_up, 1)
                pe.wait_ge(steps_down, 1)
                pe.matmul(ps[0:nb, 3, 32:33], upto[0:nb, 0:nb], steps_c[0:nb, :], start=True, stop=True)\
                  .then_inc(steps_up, 1)
                pe.wait_ge(passed_down, 1)
                pe.matmul(ps[:, 0, 0:n_step], ones[0:nb, :], passed[0:nb, :], start=True, stop=True)
                pe.matmul(ps[:, 1, 0:n_step], mid_w[0:nb, :], passed[0:nb, :], start=True, stop=True)\
                  .then_inc(passed_up, 1)
                pe.wait_ge(steps_made, 1)

                turn_x(early_x, 16 * (early_x // 4) + 16, 0)
                with pe.Fori(early_x // 4, (n_bin - 1) // 4) as t:
                    for u in range(4):
                        turn_x(4 * t + (u + 1), 16 * t + (32 if u == 3 else 16), (u + 1) % 4)
                        update_x(4 * t + u, u)
                update_x(n_bin - 1, 0)
                pe.wait_ge(xt_out, n_bin + 2)
                pe.wait_ge(split, 1)

                def turn(u, here, n):
                    pe.wait_ge(e_here[u], here)
                    pe.wait_ge(e_low, n)
                    for k in range(KC):
                        for j in range(T):
                            at_ = j * D + k * P
                            last = pe.transpose(ps[:, k, j * P:(j + 1) * P], e_in[:, u, at_:at_ + P],
                                                ident[:, :])
                    last.then_inc(e_turned, 1)

                PARTS = [(0, 0), (0, 1), (1, 0)]

                def hidden(u, n):
                    pe.wait_ge(e_low, n + 1)
                    pe.wait_ge(x_whole, n)
                    for m in range(KC):
                        for k in range(KC):
                            for a, b in PARTS:
                                last = pe.matmul(ps[:, 2 + m, :], w_in[b][:, k, m * P:(m + 1) * P],
                                                 e_t[a][:, u, k, :], start=(k == 0 and a + b == 0),
                                                 stop=(k == KC - 1 and a == 1))
                    last.then_inc(x_up, 1)

                def values(u, n):
                    pe.wait_ge(x_low, n + 2)
                    pe.wait_ge(va_taken, n + 1)
                    for j in range(T):
                        for k in range(KC):
                            for a, b in PARTS:
                                last = pe.matmul(ps[:, 4 + j, 0:VA], x_t[a][:, u, k, j * P:(j + 1) * P],
                                                 w_va[b][:, k, :], start=(k == 0 and a + b == 0),
                                                 stop=(k == KC - 1 and a == 1))
                    last.then_inc(va_up, 1)

                turn(0, 16, 0)
                turn(1, 16, 1)
                hidden(0, 0)
                with pe.Fori(0, n_block // 4 - 1) as t:
                    for u in range(4):
                        turn((u + 2) % 4, 16 * t + (16 if u < 2 else 32), 4 * t + (u + 2))
                        hidden((u + 1) % 2, 4 * t + (u + 1))
                        values(u % 2, 4 * t + u)
                for n in range(n_block - 4, n_block - 2):
                    turn((n + 2) % 4, 16 * ((n + 2) // 4) + 16, n + 2)
                    hidden((n + 1) % 2, n + 1)
                    values(n % 2, n)
                hidden(1, n_block - 1)
                values(0, n_block - 2)
                values(1, n_block - 1)

                def turn_hot(n, u):
                    v = u % 2
                    pe.wait_ge(hot_a, n + 1)
                    pe.wait_ge(hot_b, n + 1)
                    pe.wait_ge(hot_c, n + 1)
                    pe.wait_ge(hot_t_here, n + 1)
                    for j in range(T):
                        last = pe.transpose(ps[:, v, j * P:(j + 1) * P], hot[:, u, j, :], ident[:, :])
                    last.then_inc(hot_turned, 1)

                def edge_shifts(n, u):
                    v = u % 2
                    b = pe.value_load(bin_of_i[0:1, ds(n, 1)], min_val=0, max_val=n_bin)
                    pe.wait_ge(hot_t_here, n + 2)
                    pe.wait_ge(v_off, n + 1)
                    for j in range(T):
                        last = pe.matmul(ps[:, 2 + v, j * H:(j + 1) * H], hot_t[:, v, j, :], shift[:, b, :],
                                         start=True, stop=True)
                    last.then_inc(shift_up, 1)

                def sums(n, u):
                    pe.wait_ge(hot_a, n + 1)
                    pe.wait_ge(hot_b, n + 1)
                    pe.wait_ge(hot_c, n + 1)
                    pe.wait_ge(wv_made, n + 1)
                    pe.wait_ge(sums_added, n + 1)
                    for j in range(T):
                        last = pe.matmul(ps[:, 4 + u, 0:VA], hot[:, u, j, :], wv[:, u, j, :],
                                         start=(j == 0), stop=(j == T - 1))
                    last.then_inc(sums_up, 1)

                pe.wait_ge(wide_known, 1)
                far = pe.value_load(wide[0:1, 0:1], min_val=0, max_val=1)
                with pe.If(far > 0):
                    with pe.Fori(0, n_step) as i:
                        for j in range(T):
                            pe.wait_ge(outside_made, i + 1)
                            pe.wait_ge(spread_made, T * i + (j + 1))
                            for g in range(2):
                                pe.matmul(ps[:, g, :], outside[:, j, :],
                                          far_ident[:, :].unsqueeze(1).to_broadcast([P, H // 2, P]),
                                          start=True, stop=False)
                                last = pe.matmul(ps[:, g, :], ones[:, :],
                                                 spread[:, g * H // 2:(g + 1) * H // 2, :],
                                                 start=False, stop=True)
                            last.then_inc(scores_up, 1)
                    pe.wait_ge(shifts_known, 1)
                    turn_hot(0, 0)
                    edge_shifts(0, 0)
                    sums(0, 0)
                    with pe.Fori(0, (n_step - 1) // 4) as q:
                        for u in range(4):
                            turn_hot(4 * q + (u + 1), (u + 1) % 4)
                            edge_shifts(4 * q + (u + 1), (u + 1) % 4)
                            sums(4 * q + (u + 1), (u + 1) % 4)
                with pe.Else():
                    sums(0, 0)
                    with pe.Fori(0, (n_step - 1) // 4) as q:
                        for u in range(4):
                            sums(4 * q + (u + 1), (u + 1) % 4)

                def turn_rows(of, ready, n, turned):
                    pe.wait_ge(ready, n + 1)
                    for b0, b1 in halves:
                        for b in range(b0, b1):
                            for k in range(KC):
                                a = (b * KC + k) * P
                                last = pe.transpose(ps[:, a // BANK, a % BANK:a % BANK + P],
                                                    of[:, b, k * P:(k + 1) * P], ident[:, :])
                        last.then_inc(turned, 1)

                def product(left, w, n, here, bias, up):
                    for h, (b0, b1) in enumerate(halves):
                        pe.wait_ge(here, 2 * n + (h + 3))
                        for b in range(b0, b1):
                            a = b * D
                            to = ps[:, 4 + a // BANK, a % BANK:a % BANK + D]
                            for k in range(KC):
                                last = pe.matmul(to, left[:, b * KC + k, :], w[:, k, :],
                                                 start=(k == 0), stop=(k == KC - 1 and bias is None))
                            if bias is not None:
                                pe.matmul(to, one_row[:, :], bias[0][:, :], start=False, stop=False)
                                last = pe.matmul(to, one_row[:, :], bias[1][:, :], start=False, stop=True)
                    last.then_inc(up, 1)

                def first(n):
                    if not isinstance(n, int) or n:
                        pe.wait_ge(z_t_here, 2 * n)
                    turn_rows(y, normed[0], n, y_turned)
                    if not isinstance(n, int) or n:
                        pe.wait_ge(up2_here, n)
                    product(y_t, w_rff, n, y_t_here, bias_parts, product1)

                def second(n):
                    pe.wait_ge(y_t_here, 2 * n + 6)
                    turn_rows(z, normed[1], n, z_turned)
                    pe.wait_ge(up1_here, n + 3)
                    product(z_t, w_upd, n, z_t_here, None, product2)

                pe.wait_ge(sums_added, n_step + 4)
                first(0)
                pe.wait_ge(up1_here, 2)
                pe.wait_ge(y_t_here, 4)
                first(1)
                second(0)
                with pe.Fori(2, n_batch) as k:
                    first(k)
                    second(k - 1)
                turn_rows(z, normed[1], n_batch - 1, z_turned)
                pe.wait_ge(up2_here, n_batch)
                product(z_t, w_upd, n_batch - 1, z_t_here, None, product2)

            @block.vector
            def _(vec):
                done = [0]

                def link(ins):
                    done[0] += 1
                    ins.then_inc(v_link, 1)
                    vec.wait_ge(v_link, done[0])

                vec.nop().then_inc(sums_added, 4)
                vec.nop().then_inc(v_off, 2)
                vec.nop().then_inc(va_taken, 1)
                vec.nop().then_inc(meta_used, 1)
                vec.nop().then_inc(x_low, 1)
                vec.nop().then_inc(z_read, 1)
                vec.nop().then_inc(res_made, 1)
                vec.wait_ge(consts, 6)
                vec.tensor_scalar(ident[:, :], diff[:, :], 0.0, None, ALU.is_equal)
                vec.tensor_scalar(before[:, :], diff[:, :], 0.0, None, ALU.is_gt)
                vec.tensor_scalar(far_ident[:, :], diff[:, :], 0.0, -FAR, ALU.is_equal, ALU.mult)
                vec.tensor_scalar(upto[:, :], diff[:, :], 0.0, None, ALU.is_ge).then_inc(consts_made, 1)
                vec.wait_ge(src_in, 48)
                vec.tensor_copy(src_f[0:half, :, :], src_i[0:half, :, :]).then_inc(src_cast, 1)
                vec.memset(place, float(2 * n_row))
                vec.wait_ge(wk_in, 128)
                vec.tensor_tensor(fold[:, 0:KC, :], raw_k[:, :, :],
                                  att[:, :].unsqueeze(1).to_broadcast([P, KC, D]), ALU.mult)
                link(vec.tensor_tensor(fold[:, KC, :], b_k, att[:, :], ALU.mult))
                for k in range(KC):
                    vec.tensor_reduce(raw_va[:, k, D:VA], fold[:, k, :].rearrange("p (h c) -> p h c", h=H),
                                      AX.X, ALU.add)
                vec.tensor_reduce(b_va[:, D:VA], fold[:, KC, :].rearrange("p (h c) -> p h c", h=H),
                                  AX.X, ALU.add).then_inc(folded, 1)
                vec.wait_ge(src_turned, 1)
                for s in range(2):
                    last = vec.tensor_copy(seg_f[:, s * half:(s + 1) * half, :],
                                           ps[:, s, 0:T * half].rearrange("p (t b) -> p b t", t=T))
                link(last)
                link(vec.memset(seg_f[0:repeated // T, n_block - 1, :], float(P * (n_bin + 1))))
                link(vec.tensor_copy(seg_i, seg_f[:, :, :].rearrange("p b t -> p (b t)")))
                link(vec.tensor_scalar(bin_i, seg_i, P.bit_length() - 1, None,
                                       ALU.logical_shift_right))
                link(vec.tensor_copy(bin_h[:, :], bin_i))
                for b in range(n_bin):
                    vec.tensor_scalar(mask[:, b, :], bin_h[:, :], float(b), None, ALU.is_equal)\
                       .then_inc(masks_made, 1)
                for n, b in enumerate(vec_bins):
                    vec.wait_ge(masks_made, b + 1)
                    vec.tensor_reduce(count[:, b:b + 1], mask[:, b, :], AX.X, ALU.add).then_inc(counted_too, 1)
                vec.wait_ge(folded, 1)
                vec.wait_ge(params_in, 16 * (len(params) + len(rows_of)))
                vec.tensor_copy(one_row[:, :], ones[0:1, :])
                for parts, raw in ((bias_parts, bias_row), (w_in, raw_in), (w_va, raw_va)):
                    whole = (slice(None),) * len(raw.shape)
                    link(vec.tensor_copy(parts[0][whole], raw[whole]))
                    last = vec.tensor_tensor(parts[1][whole], raw[whole], parts[0][whole].bitcast(FP32),
                                             ALU.subtract)
                last.then_inc(split, 1)
                vec.memset(hi[:, :, :], -3.0e38)
                vec.memset(lo[:, :, :], 3.0e38).then_inc(v_score, 1)
                vec.wait_ge(totals_up, 1)
                vec.tensor_copy(tot_c[0:n_bin, :], ps[0:n_bin, 2, 128:129]).then_inc(tot_c_down, 1)
                link(vec.tensor_copy(total[:, :], ps[:, 2, 64:64 + n_bin]))
                link(vec.tensor_tensor_scan(upto_bin[:, :], total[:, :], total[:, :], 0.0, ALU.add, ALU.bypass))
                link(vec.tensor_tensor(start_at[:, :], upto_bin[:, :], total[:, :], ALU.subtract))
                vec.tensor_tensor(start_at[:, :], start_at[:, :], ps[:, 2, 0:n_bin], ALU.add)\
                   .then_inc(starts_made, 1)
                nb = n_bin
                vec.wait_ge(ends_up, 1)
                vec.tensor_scalar(ends_i[0:nb, 0:1], ps[0:nb, 3, 16:17], float(BLOCK - 1), None, ALU.add)
                vec.tensor_copy(ends_i[0:nb, 1:2], ps[0:nb, 3, 17:18])
                link(vec.tensor_copy(ends_i[0:nb, 2:3], ps[0:nb, 3, 16:17]))
                lb = BLOCK.bit_length() - 1
                vec.tensor_scalar(ends_i[0:nb, 4:6], ends_i[0:nb, 0:2], lb, None, ALU.logical_shift_right)
                link(vec.tensor_scalar(ends_i[0:nb, 6:7], ends_i[0:nb, 2:3], BLOCK - 1, None, ALU.bitwise_and))
                link(vec.tensor_copy(ends[0:nb, 0:3], ends_i[0:nb, 4:7]))
                vec.tensor_tensor(steps_c[0:nb, :], ends[0:nb, 0:1], ends[0:nb, 1:2], ALU.subtract)\
                   .then_inc(steps_down, 1)
                link(vec.tensor_scalar(mid[0:nb, :], ends[0:nb, 2:3], 1.0, None, ALU.min))
                vec.tensor_scalar(mid_w[0:nb, :], ones[0:nb, :], mid[0:nb, 0:1], None, ALU.mult)
                vec.wait_ge(steps_up, 1)
                link(vec.tensor_copy(steps_in[0:nb, :], ps[0:nb, 3, 32:33]))
                vec.tensor_scalar(passed[0:nb, :], step_no[0:nb, :], steps_in[0:nb, 0:1], None, ALU.is_ge)\
                   .then_inc(passed_down, 1)
                vec.wait_ge(passed_up, 1)
                vec.tensor_copy(bin_of[:, :], ps[:, 0, 0:n_step])
                link(vec.tensor_tensor(group_of[:, :], step_no[:, :], ps[:, 1, 0:n_step], ALU.subtract))
                vec.tensor_scalar(first_seg[:, :], bin_of[:, :], float(P), None, ALU.mult)
                vec.tensor_copy(bin_of_i[:, :], bin_of[:, :])
                vec.tensor_scalar(group_of_i[:, :], group_of[:, :], float(n_block - 1), 0.0, ALU.min, ALU.max)\
                   .then_inc(steps_made, 1)
                def edges_low(n, u):
                    vec.wait_ge(e_high, n + 1)
                    for k in range(KC):
                        last = vec.tensor_tensor(e_t[1][:, u, k, :], ps[:, k, :],
                                                 e_t[0][:, u, k, :].bitcast(FP32), ALU.subtract)
                    last.then_inc(e_low, 1)

                def hidden_low(n, u):
                    vec.wait_ge(x_whole, n + 1)
                    vec.tensor_tensor(x_t[1][:, u, :, :], x_f[:, :, :], x_t[0][:, u, :, :].bitcast(FP32),
                                      ALU.subtract).then_inc(x_low, 1)

                vec.wait_ge(starts_made, 1)
                def run(n):
                    if n >= 4:
                        vec.wait_ge(puts_made, n - 3)
                    vec.tensor_tensor_scan(runs[:, n % 4, :], mask[:, turn_of(n), :], mask[:, turn_of(n), :],
                                           start_at[:, turn_of(n):turn_of(n) + 1], ALU.add, ALU.bypass)\
                       .then_inc(runs_made, 1)

                def put(n):
                    vec.wait_ge(runs_made, n + 1)
                    if n:
                        vec.wait_ge(puts_made, n)
                    vec.copy_predicated(place, mask[:, turn_of(n), :], runs[:, n % 4, :]).then_inc(puts_made, 1)

                run(0)
                for n in range(n_bin):
                    if n + 1 < n_bin:
                        run(n + 1)
                    put(n)
                    if n == n_bin - 12:
                        edges_low(0, 0)
                    if n == n_bin - 8:
                        edges_low(1, 1)
                    if n == n_bin - 4:
                        hidden_low(0, 0)
                vec.wait_ge(puts_made, n_bin)
                vec.tensor_scalar(place_i[:, :], place, -1.0, None, ALU.add).then_inc(tables, 1)
                def take_values(t, u):
                    vec.wait_ge(va_up, 2 * t + (u + 3))
                    if not isinstance(t, int) or t:
                        vec.wait_ge(sent[u], 16 * T * t)
                    vec.tensor_tensor(row[:, u, :, 0:VA], ps[:, 4:8, 0:VA],
                                      b_va[:, :].unsqueeze(1).to_broadcast([P, T, VA]), ALU.add)\
                       .then_inc(va_taken, 1)
                    vec.wait_ge(va_taken, 2 * t + (u + 2))
                    s = row[:, u, :, D:VA]
                    vec.scalar_tensor_tensor(s, s, SLOPE, s, ALU.mult, ALU.max).then_inc(row_ready, 1)
                    vec.wait_ge(row_ready, 2 * t + (u + 1))
                    vec.wait_ge(v_score, 2 * t + (u + 1))
                    vec.tensor_tensor(hi[:, :, :], hi[:, :, :], s, ALU.max)
                    vec.tensor_tensor(lo[:, :, :], lo[:, :, :], s, ALU.min).then_inc(v_score, 1)

                for u in range(2):
                    edges_low(u + 2, u)
                    hidden_low(u + 1, 1 - u)
                    take_values(0, u)
                with vec.Fori(1, n_block // 2 - 1) as t:
                    for u in range(2):
                        edges_low(2 * t + (u + 2), u)
                        hidden_low(2 * t + (u + 1), 1 - u)
                        take_values(t, u)
                hidden_low(n_block - 1, 1)
                for u in range(2):
                    take_values(n_block // 2 - 1, u)

                vec.wait_ge(v_score, n_block + 1)
                vec.tensor_reduce(ext[:, 0:H], hi[:, :, :].rearrange("p t h -> p h t"), AX.X, ALU.max)
                link(vec.tensor_reduce(ext[:, H:2 * H], lo[:, :, :].rearrange("p t h -> p h t"), AX.X, ALU.min))
                vec.tensor_scalar(ext[:, H:2 * H], ext[:, H:2 * H], -1.0, None, ALU.mult).then_inc(ext_ready, 1)
                vec.wait_ge(ext_reduced, 1)
                link(vec.tensor_reduce(top[:, :], ext_all[:, :].rearrange("p (a h) -> p a h", h=H), AX.X, ALU.max))
                vec.tensor_scalar(minus_top[:, :], top[:, 0:1], -1.0, None, ALU.mult)
                vec.tensor_scalar(wide[:, :], top[:, 1:2], top[:, 0:1], SPAN, ALU.add, ALU.is_gt)\
                   .then_inc(wide_known, 1)
                vec.wait_ge(wide_known, 1)
                far = vec.value_load(wide[0:1, 0:1], min_val=0, max_val=1)

                def hot_first(n, here, u):
                    vec.wait_ge(sums_up, n + 1)
                    vec.wait_ge(loaded_in[u], here)
                    vec.tensor_scalar(hot[:, u, 0, :], col[:, :], first_seg[:, ds(n, 1)],
                                      loaded[:, u, 0, VA:ROW], ALU.add, ALU.is_equal).then_inc(hot_a, 1)

                def far_offsets(n, here, u):
                    v = u % 2
                    vec.wait_ge(loaded_in[u], here)
                    vec.wait_ge(shift_up, n + 3)
                    vec.tensor_tensor(off[:, v, :, :], loaded[:, u, :, D:VA],
                                      ps[:, 2 + v, 0:T * H].rearrange("p (t h) -> p t h", t=T), ALU.subtract)\
                       .then_inc(v_off, 1)
                    vec.wait_ge(v_off, n + 3)
                    vec.tensor_scalar(off[:, v, :, :], off[:, v, :, :], 0.0, None, ALU.min).then_inc(off_made, 1)

                def weigh(n, u):
                    vec.wait_ge(exp_made, n + 1)
                    vec.tensor_tensor(
                        wv[:, u, :, 0:D].rearrange("p t (h c) -> p t h c", h=H),
                        loaded[:, u, :, 0:D].rearrange("p t (h c) -> p t h c", h=H),
                        wv[:, u, :, D:VA].unsqueeze(3).to_broadcast([P, T, H, C]), ALU.mult)\
                       .then_inc(wv_made, 1)

                def add_sums(n, u):
                    b = vec.value_load(bin_of_i[0:1, ds(n, 1)], min_val=0, max_val=n_bin)
                    vec.wait_ge(sums_up, n + 5)
                    vec.wait_ge(sums_added, n + 4)
                    vec.tensor_tensor(acc[:, b, :], acc[:, b, :], ps[:, 4 + u, 0:VA], ALU.add)\
                       .then_inc(sums_added, 1)

                vec.wait_ge(acc_clear, n_bin + 1)
                with vec.If(far > 0):
                    vec.memset(shift[:, :, :], FAR).then_inc(v_max, 1)
                    with vec.Fori(0, n_step) as i:
                        b = vec.value_load(bin_of_i[0:1, ds(i, 1)], min_val=0, max_val=n_bin)
                        vec.wait_ge(meta_in, 16 * i + 16)
                        vec.tensor_tensor(seg_m[:, :], meta[:, :, H],
                                          first_seg[:, ds(i, 1)].to_broadcast([P, T]), ALU.subtract)\
                           .then_inc(v_max, 1)
                        vec.wait_ge(v_max, (2 + T) * i + 2)
                        for j in range(T):
                            last = vec.tensor_scalar(outside[:, j, :], col[:, :], seg_m[:, j:j + 1], -1.0,
                                                     ALU.not_equal, ALU.mult)
                        last.then_inc(outside_made, 1)
                        for j in range(T):
                            vec.tensor_tensor(spread, ident[:, :].unsqueeze(1).to_broadcast([P, H, P]),
                                              meta[:, j, 0:H].unsqueeze(2).to_broadcast([P, H, P]),
                                              ALU.mult).then_inc(spread_made, 1)
                            vec.wait_ge(scores_up, T * i + (j + 1))
                            vec.tensor_reduce(seg_max[:, :],
                                              ps[:, 0:2, :].rearrange("p g (h e) -> p (g h) e", e=P),
                                              AX.X, ALU.max).then_inc(v_max, 1)
                            vec.wait_ge(v_max, (2 + T) * i + (3 + j))
                            last = vec.tensor_tensor(shift[:, b, :], shift[:, b, :], seg_max[:, :], ALU.max)
                        last.then_inc(v_max, 1)
                        vec.nop().then_inc(meta_used, 1)
                    vec.memset(mid[:, :], 1.0).then_inc(shifts_known, 1)

                    def far_step(n, here, u):
                        hot_first(n, here, u)
                        far_offsets(n, here, u)
                        weigh(n, u)
                        add_sums(n, u)

                    far_step(0, 16, 0)
                    with vec.Fori(0, (n_step - 1) // 4) as q:
                        for u in range(4):
                            far_step(4 * q + (u + 1), 16 * q + (32 if u == 3 else 16), (u + 1) % 4)
                with vec.Else():
                    hot_first(0, 16, 0)
                    weigh(0, 0)
                    for n in range(1, 5):
                        hot_first(n, 16 * (n // 4) + 16, n % 4)
                        weigh(n, n % 4)
                        if n >= 2:
                            add_sums(n - 2, n - 2)
                    with vec.Fori(1, (n_step - 1) // 4) as q:
                        for u in range(4):
                            n = 4 * q + (u + 1)
                            hot_first(n, 16 * q + (32 if u == 3 else 16), (u + 1) % 4)
                            weigh(n, (u + 1) % 4)
                            add_sums(4 * q + (u - 1), (u - 1) % 4)
                    for n in range(n_step - 2, n_step):
                        add_sums(n, n % 4)

                vec.wait_ge(sums_added, n_step + 4)
                done5 = [0, 0]

                def link5(ins, k=0):
                    done5[0] += 1
                    ins.then_inc(v_link5, 1)
                    vec.wait_ge(v_link5, done5[0] + k)

                def measure(of, w, k):
                    for b in range(batch):
                        last = vec.bn_stats(stats[:, w, b, :], of[:, b, :])
                    link5(last, k)
                    vec.memset(pause[:, 1:2], 0.0)
                    for b in range(batch):
                        last = vec.bn_aggr(mv[:, w, b, :], stats[:, w, b, :])
                    last.then_inc(var_ready, 1)

                def norm(of, w, n, k):
                    vec.wait_ge(root_made, n + 1)
                    link5(vec.reciprocal(rstd[:, w, :], sd[:, w, :]), k)
                    for b in range(batch):
                        last = vec.tensor_scalar(of[:, b, :], of[:, b, :], mv[:, w, b, 0:1], rstd[:, w, b:b + 1],
                                                 ALU.subtract, ALU.mult)
                    last.then_inc(normed[w], 1)

                def scale_res(n, k):
                    vec.wait_ge(root_made, n + 1)
                    link5(vec.reciprocal(rstd[:, 2, :], sd[:, 2, :]), k)
                    vec.scalar_tensor_tensor(less[:, :], mv[:, 2, :, 0], -1.0, rstd[:, 2, :],
                                             ALU.mult, ALU.mult).then_inc(scale_made, 1)

                def make_y(k, off_=0):
                    s = acc[:, ds(k * batch, batch), :]
                    link5(vec.tensor_scalar(den[:, :, :], s[:, :, D:VA], DENOM_MIN, None, ALU.max), off_)
                    link5(vec.reciprocal(rec[:, :, :], den[:, :, :]), off_)
                    if not isinstance(k, int) or k:
                        vec.wait_ge(y_res_made, k)
                        vec.wait_ge(y_turned, 2 * k)
                    link5(vec.tensor_tensor(y.rearrange("p b (h c) -> p b h c", h=H),
                                            s[:, :, 0:D].rearrange("p b (h c) -> p b h c", h=H),
                                            rec[:, :, :].unsqueeze(3).to_broadcast([P, batch, H, C]), ALU.mult),
                          off_)
                    link5(vec.tensor_tensor(y, y, att[:, :].unsqueeze(1).to_broadcast([P, batch, D]), ALU.add),
                          off_)
                    measure(y, 0, off_)

                def make_z(k, off_=0):
                    vec.wait_ge(up1_here, k + 2)
                    vec.wait_ge(y_res_made, k + 1)
                    if not isinstance(k, int) or k:
                        vec.wait_ge(z_turned, 2 * k)
                    vec.scalar_tensor_tensor(z, up1, 0.0, y_res, ALU.max, ALU.add).then_inc(z_read, 1)
                    vec.wait_ge(z_read, k + 2)
                    measure(z, 1, off_)

                def make_res(k, off_=0):
                    vec.wait_ge(updated, k + 1)
                    vec.wait_ge(xr_here, 16 * k + 16 if not isinstance(k, int) or k < n_batch - 1
                                else 16 * n_batch + 16)
                    if not isinstance(k, int) or k:
                        vec.wait_ge(res_sent, 16 * k)
                    vec.scalar_tensor_tensor(res, up2, 0.0, xr, ALU.max, ALU.add).then_inc(res_made, 1)
                    vec.wait_ge(res_made, k + 2)
                    measure(res, 2, off_)

                make_y(0)
                norm(y, 0, 0, 0)
                make_y(1)
                norm(y, 0, 1, 0)
                make_z(0)
                norm(z, 1, 2, 0)
                LINKS = 10
                with vec.Fori(2, n_batch) as k:
                    begin = done5[0]
                    step_ = LINKS * (k - 2)
                    make_y(k, step_)
                    make_z(k - 1, step_)
                    norm(y, 0, 3 * k - 3, step_)
                    norm(z, 1, 3 * k - 2, step_)
                    make_res(k - 2, step_)
                    scale_res(3 * k - 1, step_)
                    assert done5[0] - begin == LINKS
                done5[0] += LINKS * (n_batch - 3)
                make_z(n_batch - 1)
                norm(z, 1, 3 * n_batch - 3, 0)
                make_res(n_batch - 2)
                scale_res(3 * n_batch - 2, 0)
                make_res(n_batch - 1)
                scale_res(3 * n_batch - 1, 0)


_INS = ["x", "src", "edge_attr_256", "L0_gnn_W_v2e", "L0_gnn_b_v2e", "L0_gnn_W_K", "L0_gnn_b_K",
        "L0_gnn_W_V", "L0_gnn_b_V", "L0_gnn_att_r", "L0_gnn_ln0_g", "L0_gnn_ln0_b", "L0_gnn_ln1_g",
        "L0_gnn_ln1_b", "L0_gnn_W_rff", "L0_gnn_b_rff", "L0_gnn_W_upd", "L0_gnn_b_upd"]


def kernel(**inputs):
    import numpy as np
    import concourse.bacc as bacc
    from concourse.bass_utils import run_bass_kernel_spmd

    nc = bacc.Bacc("TRN2", target_bir_lowering=False, num_devices=1)
    arrays, args = {}, []
    for name in _INS:
        a = np.ascontiguousarray(inputs[name])
        arrays[f"in_{name}"] = a
        args.append(nc.dram_tensor(f"in_{name}", a.shape, mybir.dt.from_np(a.dtype), kind="ExternalInput").ap())
    args.append(nc.dram_tensor("out_0", inputs["x"].shape, FP32, kind="ExternalOutput").ap())
    gnn_kernel(nc, *args)
    r = run_bass_kernel_spmd(nc, [arrays], core_ids=[0])
    return r.results[0]["out_0"]
```
